# Optimizing a Trainium2 kernel written in Bass

```python
import numpy as np
import jax
import jax.numpy as jnp

def _softmax(x, axis=-1):
    return jax.nn.softmax(x, axis=axis)

def _gelu(x):
    return jax.nn.gelu(x, approximate=True)

def _silu(x):
    return jax.nn.silu(x)

def _sigmoid(x):
    return jax.nn.sigmoid(x)

def _layernorm(x, axis=-1, eps=1e-05):
    m = jnp.mean(x, axis=axis, keepdims=True)
    v = jnp.var(x, axis=axis, keepdims=True)
    return (x - m) / jnp.sqrt(v + eps)

def _scatter_add(tgt, idx, src, axis=0):
    return tgt.at[idx].add(src)

def _segment_sum(src, seg, n):
    return jax.ops.segment_sum(src, seg, n)
kernel_name = 'mk_flamingo_gated_d1_seqx_r2_4f3292'

def setup_inputs(seed: int=0):
    np.random.seed(seed)
    _w = jnp.asarray

    def _rec_inputs():
        import jax
        import jax.numpy as jnp
        _rk = jax.random.key(seed)
        x = 0.0001212 + 1 * jax.random.normal(jax.random.fold_in(_rk, 1), (4, 1024, 1024), jnp.float32)
        _lenS = 1024 - jax.random.randint(jax.random.fold_in(_rk, 7), (4,), 0, max(1, 1024 // 4) + 1, jnp.int32)
        _lenS2 = 1024 - jax.random.randint(jax.random.fold_in(_rk, 8), (4,), 0, max(1, 1024 // 4) + 1, jnp.int32)
        _ctx_2048P = jax.random.normal(jax.random.fold_in(_rk, 11), (4, 16, 1024), jnp.float32)
        _ctx_2048c = jax.random.dirichlet(jax.random.fold_in(_rk, 511), 0.3 * jnp.ones((16,), jnp.float32), (4, 1024))
        _ctx_2048t = jnp.einsum('bsk,bkd->bsd', _ctx_2048c, _ctx_2048P)
        _ctx_2048t = _ctx_2048t * jax.lax.rsqrt(jnp.mean(jnp.square(_ctx_2048t)) + 1e-12) * 0.953939
        ctx_2048 = 0.000173663 + 1.0001 * (_ctx_2048t + 0.3 * jax.random.normal(jax.random.fold_in(_rk, 611), (4, 1024, 1024), jnp.float32))
        _g = jax.random.normal(jax.random.fold_in(_rk, 9001), (2, 1), jnp.float32)
        _g = jnp.sign(_g) * jnp.maximum(jnp.abs(_g), 1.0) + (_g == 0) * 1.0
        g_xattn = _g[0]
        g_ffn = _g[1]
        return (x, ctx_2048, g_xattn, g_ffn)
    x, ctx_2048, g_xattn, g_ffn = _rec_inputs()

    def _L0_xattn_setup():
        import jax, jax.numpy as jnp
        import numpy as np
        B_DIM, T_DIM, C_DIM = (16, 512, 1024)

        def _wkv(w, u, k, v):
            Bn, Tn, Cn = k.shape
            NEG_INF = jnp.float32(-1e+38)

            def step(carry, kv_t):
                p, q, o = carry
                kt, vt = kv_t
                no = jnp.maximum(o, u + kt)
                A = jnp.exp(o - no)
                E = jnp.exp(u + kt - no)
                y = (A * p + E * vt) / (A * q + E)
                no2 = jnp.maximum(w + o, kt)
                A2 = jnp.exp(w + o - no2)
                E2 = jnp.exp(kt - no2)
                return ((A2 * p + E2 * vt, A2 * q + E2, no2), y)
            init = (jnp.zeros((Bn, Cn), k.dtype), jnp.zeros((Bn, Cn), k.dtype), jnp.full((Bn, Cn), NEG_INF, k.dtype))
            kT = jnp.moveaxis(k, 1, 0)
            vT = jnp.moveaxis(v, 1, 0)
            _, yT = jax.lax.scan(step, init, (kT, vT))
            return jnp.moveaxis(yT, 0, 1)
        key = jax.random.key(seed)
        k1, k2, k3, k4 = jax.random.split(key, 4)
        w = -jnp.exp(jax.random.normal(k1, (C_DIM,), jnp.float32))
        u = jax.random.normal(k2, (C_DIM,), jnp.float32)
        k = jax.random.normal(k3, (B_DIM, T_DIM, C_DIM), jnp.float32)
        v = jax.random.normal(k4, (B_DIM, T_DIM, C_DIM), jnp.float32)
        return {'B': B_DIM, 'T': T_DIM, 'C': C_DIM, 'w': w, 'u': u, 'k': k, 'v': v}
    _L0_xattn_all = _L0_xattn_setup()
    _L0_xattn_in = {k: v for k, v in _L0_xattn_all.items() if k in ('w', 'u')}
    del _L0_xattn_all

    def _L0_ffn_setup():
        import jax, jax.numpy as jnp
        import numpy as np
        key = jax.random.key(seed)
        k1, k2, k3, k4, k5 = jax.random.split(key, 5)
        B, L, H, N = (2, 1024, 1024, 4096)
        x = jax.random.normal(k1, (B, L, H), dtype=jnp.float32)
        W0 = jax.random.normal(k2, (N, H), dtype=jnp.float32) * (1.0 / np.sqrt(H))
        bias0 = jax.random.normal(k3, (N,), dtype=jnp.float32) * 0.02
        W1 = jax.random.normal(k4, (H, N), dtype=jnp.float32) * (1.0 / np.sqrt(N))
        bias1 = jax.random.normal(k5, (H,), dtype=jnp.float32) * 0.02
        return {'x': x, 'W0': W0, 'bias0': bias0, 'W1': W1, 'bias1': bias1}
    _L0_ffn_all = _L0_ffn_setup()
    _L0_ffn_in = {k: v for k, v in _L0_ffn_all.items() if k in ('W0', 'bias0', 'W1', 'bias1')}
    del _L0_ffn_all
    return {'x': x, 'ctx_2048': ctx_2048, 'g_xattn': g_xattn, 'g_ffn': g_ffn, 'L0_xattn_w': _L0_xattn_in['w'], 'L0_xattn_u': _L0_xattn_in['u'], 'L0_ffn_W0': _L0_ffn_in['W0'], 'L0_ffn_bias0': _L0_ffn_in['bias0'], 'L0_ffn_W1': _L0_ffn_in['W1'], 'L0_ffn_bias1': _L0_ffn_in['bias1']}

def reference(x, ctx_2048, g_xattn, g_ffn, L0_xattn_w, L0_xattn_u, L0_ffn_W0, L0_ffn_bias0, L0_ffn_W1, L0_ffn_bias1):
    import jax
    import jax.numpy as jnp

    def _L0_xattn_ref(B, T, C, w, u, k, v):
        import jax, jax.numpy as jnp
        import numpy as np
        B_DIM, T_DIM, C_DIM = (16, 512, 1024)

        def _wkv(w, u, k, v):
            Bn, Tn, Cn = k.shape
            NEG_INF = jnp.float32(-1e+38)

            def step(carry, kv_t):
                p, q, o = carry
                kt, vt = kv_t
                no = jnp.maximum(o, u + kt)
                A = jnp.exp(o - no)
                E = jnp.exp(u + kt - no)
                y = (A * p + E * vt) / (A * q + E)
                no2 = jnp.maximum(w + o, kt)
                A2 = jnp.exp(w + o - no2)
                E2 = jnp.exp(kt - no2)
                return ((A2 * p + E2 * vt, A2 * q + E2, no2), y)
            init = (jnp.zeros((Bn, Cn), k.dtype), jnp.zeros((Bn, Cn), k.dtype), jnp.full((Bn, Cn), NEG_INF, k.dtype))
            kT = jnp.moveaxis(k, 1, 0)
            vT = jnp.moveaxis(v, 1, 0)
            _, yT = jax.lax.scan(step, init, (kT, vT))
            return jnp.moveaxis(yT, 0, 1)
        return _wkv(w, u, k, v)

    def _L0_ffn_ref(x, W0, bias0, W1, bias1):
        import jax, jax.numpy as jnp
        import numpy as np
        B, L, H = x.shape
        X = x.reshape(-1, H).astype(jnp.float16)
        D = jnp.dot(X.astype(jnp.float32), W0.T) + bias0
        D = jax.nn.gelu(D, approximate=False).astype(jnp.float16)
        E = jnp.dot(D.astype(jnp.float32), W1.T) + bias1
        return E.astype(jnp.float16).reshape(B, L, H)
    x = x + jnp.tanh(g_xattn[0]) * _L0_xattn_ref(4, 1024, 1024, L0_xattn_w, L0_xattn_u, _layernorm(x, axis=-1), ctx_2048)
    x = x + jnp.tanh(g_ffn[0]) * _L0_ffn_ref(_layernorm(x, axis=-1), L0_ffn_W0, L0_ffn_bias0, L0_ffn_W1, L0_ffn_bias1)
    return x

_drawn_inputs = setup_inputs


def setup_inputs(seed=0):
    import zlib

    import numpy as np

    out = dict(_drawn_inputs(seed))
    spreads = {}
    factors = {'L0_ffn_bias0': 6.154, 'L0_ffn_bias1': 4.195}
    for name, (base, spread) in spreads.items():
        noise = np.random.default_rng([zlib.crc32(name.encode()), seed]).standard_normal(out[name].shape)
        drawn = base * np.exp(spread * noise) if base else spread * noise
        out[name] = jnp.asarray(drawn.astype(out[name].dtype))
    for name, factor in factors.items():
        out[name] = (out[name] * factor).astype(out[name].dtype)
    return out
```

```python
from contextlib import ExitStack

import numpy as np
import concourse.bass as bass
from concourse import mybir

ALU = mybir.AluOpType
ACT = mybir.ActivationFunctionType
F32 = mybir.dt.float32
F16 = mybir.dt.float16

P = 128
B, L, H, N = 4, 1024, 1024, 4096
CB = H // P
TILES = L // P
HALF = 512
HT = HALF // P
UNITS = 2 * CB
NB = N // P
Q = 4
STEPS = NB // Q
assert STEPS == CB == 8 and TILES == 8
GROUPS1 = 2 * NB
GROUPS = GROUPS1 + 2 * CB
BANKS = 4
EPS = 1e-5
NEG_INF = -1e38
R_CAP = 60.0
W_SCALE = 1024.0


def groups_through(b, step):
    if step < STEPS:
        return GROUPS * b + 2 * Q * (step + 1)
    return GROUPS * b + GROUPS1 + 2 * (step - STEPS + 1)


def groups_through_0(v):
    if v < 2 * STEPS:
        return Q * (v + 1)
    return GROUPS1 + 2 * (v - 2 * STEPS + 1)


def build(nc, x, vT, g_xattn, g_ffn, w, u, w0, bias0, w1, bias1, out):
    x2_dram = nc.dram_tensor("x2_dram", (B, CB, P, TILES, P), F32).ap()
    parts_dram = nc.dram_tensor("parts_dram", (2 * STEPS, P, 2 * Q * 1024), F16).ap()
    x2_view = x2_dram.rearrange("b c p t h -> b t p c h")

    with ExitStack() as ctx:
        def sb(name, shape, dt=F32):
            return ctx.enter_context(nc.sbuf_tensor(name, shape, dt))

        def ps(name, shape, dt=F32):
            return ctx.enter_context(nc.psum_tensor(name, shape, dt))

        def sem(name):
            return ctx.enter_context(nc.semaphore(name))

        def sems(name, n=2):
            return [sem(f"{name}{i}") for i in range(n)]

        ident = sb("ident", [P, P])
        ident16 = sb("ident16", [P, P], F16)
        gates = sb("gates", [P, 2])
        tg = sb("tg", [P, 2])
        power = sb("power", [P, 1])
        w_u = sb("w_u", [P, 2, UNITS])
        b0 = sb("b0", [P, NB])
        b1 = sb("b1", [P, CB])
        xin = sb("xin", [P, 2, H])
        xres = sb("xres", [P, 2, H])
        xh = sb("xh", [P, H], F16)
        stats = sb("stats", [P, 2, 2, 6])
        mv = sb("mv", [P, 2, 2])
        rstd = sb("rstd", [P, 2, 2])
        K = sb("K", [P, UNITS, HALF])
        uV = sb("uV", [P, 2, HALF])
        uOE = sb("uOE", [P, 2, 2, HALF + 1])
        uA = sb("uA", [P, 2, HALF])
        uR = sb("uR", [P, 2, HALF])
        st_o = sb("st_o", [P, UNITS + CB])
        st_pq = sb("st_pq", [P, UNITS + CB, 2])
        XT = sb("XT", [P, CB, L], F16)
        DT = sb("DT", [P, NB, L], F16)
        stage = sb("stage", [P, 2, 1024])
        W = sb("W", [P, 2, 2, Q, 1024], F16)
        e16 = sb("e16", [P, 2, HALF], F16)
        xo = sb("xo", [P, 2, TILES, P])

        acc = [ps(f"acc{i}", [P, HALF]) for i in range(BANKS)]
        trA = ps("trA", [P, CB, P])
        trX = ps("trX", [P, CB, P], F16)
        trE = ps("trE", [P, HT, P], F16)

        s_const = sem("const_landed")
        s_tg = sem("tg_ready")
        s_pool0 = sem("pool_constants")
        s_dve0 = sem("dve_constants")
        x_landed, xr_landed, v_landed = sems("x_landed"), sems("xr_landed"), sems("v_landed")
        x2_stored, xo_landed, out_stored = sems("x2_stored"), sems("xo_landed"), sems("out_stored")
        wst_landed, w_landed, w_stored = sems("wst_landed"), sems("w_landed"), sems("w_stored")
        bn_done, mv_done, ve_done, rstd_done = (sems(n) for n in ("bn_done", "mv_done", "ve_done", "rstd_done"))
        xn_ready, kt_done, k_copied = sem("xn_ready"), sem("kt_done"), sem("k_copied")
        yt_done, x2_done, xh_ready = sem("yt_done"), sem("x2_done"), sem("xh_ready")
        xt_done, xt_copied = sem("xt_done"), sem("xt_copied")
        o_seeded, o_scanned, o_saved = sem("o_seeded"), sem("o_scanned"), sem("o_saved")
        d1_done, d2_done, z_raw, z_done = sem("d1_done"), sem("d2_done"), sem("z_raw"), sem("z_done")
        e2_done, a2_done, r_done = sem("e2_done"), sem("a2_done"), sem("r_done")
        ev_done, rv_done = sem("ev_done"), sem("rv_done")
        pq_seeded, q_scanned, p_scanned, pq_saved = (sem(n) for n in ("pq_seeded", "q_scanned", "p_scanned", "pq_saved"))
        den_done, num_done, rec_done, y_done = sem("den_done"), sem("num_done"), sem("rec_done"), sem("y_done")
        hi_done, ws_done, lo_done = sem("hi_done"), sem("ws_done"), sem("lo_done")
        mm_done, acc_drained = sem("mm_done"), sem("acc_drained")
        et_done, out_added = sem("et_done"), sem("out_added")

        block = ctx.enter_context(nc.Block())

        @block.sync
        def _(sp):
            def load_x(T, slot):
                if not (isinstance(T, int) and T < 2):
                    sp.wait_ge(kt_done, T - 1)
                sp.dma_start(xin[:, slot, :], x[T]).then_inc(x_landed[slot], 16)

            def load_xr(b, tile):
                slot, T = tile % 2, TILES * b + tile
                if not (isinstance(T, int) and T < 2):
                    sp.wait_ge(x2_stored[slot], 64 * b + 16 * (tile // 2))
                    sp.wait_ge(xh_ready, T - 1)
                sp.dma_start(xres[:, slot, :], x[T]).then_inc(xr_landed[slot], 16)

            def store_x2(b, tile):
                sp.wait_ge(x2_done, TILES * b + tile + 1)
                sp.dma_start(x2_view[b, tile], xres[:, tile % 2, :].rearrange("p (c h) -> p c h", c=CB))\
                    .then_inc(x2_stored[tile % 2], 16)

            def load_v(b, pair):
                for j in range(2):
                    if not (isinstance(b, int) and isinstance(pair, int) and b == 0 and pair == 0):
                        sp.wait_ge(y_done, UNITS * b + 2 * pair + j - 1)
                    sp.dma_start(uV[:, j, :], vT[b, 2 * pair + j]).then_inc(v_landed[j], 16)

            def load_piece(g):
                if g >= 2:
                    sp.wait_ge(lo_done, g - 1)
                src = w0[g] if g < NB else w1[g - NB]
                sp.dma_start(stage[:, g % 2, :], src).then_inc(wst_landed[g % 2], 16)

            def split_step(s):
                for g in range(Q * s, Q * (s + 1)):
                    load_piece(g)

            def store_parts(s):
                sp.wait_ge(lo_done, Q * (s + 1))
                sp.dma_start(parts_dram[s], W[:, s % 2, :, :, :].rearrange("p a q n -> p (a q n)"))\
                    .then_inc(w_stored[s % 2], 16)

            def load_parts(s, slot, groups):
                sp.wait_ge(mm_done, groups)
                sp.dma_start(W[:, slot, :, :, :].rearrange("p a q n -> p (a q n)"), parts_dram[s])\
                    .then_inc(w_landed[slot], 16)

            load_x(0, 0)
            load_x(1, 1)
            sp.dma_start(w_u[:, 0, 0:CB], w).then_inc(s_const, 16)
            sp.dma_start(w_u[:, 0, CB:UNITS], w).then_inc(s_const, 16)
            sp.dma_start(w_u[:, 1, 0:CB], u).then_inc(s_const, 16)
            sp.dma_start(w_u[:, 1, CB:UNITS], u).then_inc(s_const, 16)
            sp.dma_start(gates[:, 0:1], g_xattn).then_inc(s_const, 16)
            sp.dma_start(gates[:, 1:2], g_ffn).then_inc(s_const, 16)
            sp.dma_start(b0[:, :], bias0).then_inc(s_const, 16)
            sp.dma_start(b1[:, :], bias1).then_inc(s_const, 16)
            load_v(0, 0)
            load_x(2, 0)
            load_x(3, 1)
            load_xr(0, 0)
            load_xr(0, 1)
            for item in (0, 1, "v1", 2, 3, 4, "v2", 5, 6, "v3", 7):
                if isinstance(item, int):
                    load_piece(item)
                else:
                    load_v(0, int(item[1]))
            load_x(4, 0)
            load_x(5, 1)
            for T in range(HT):
                store_x2(0, T)
                if T + 2 < HT:
                    load_xr(0, T + 2)
            store_parts(0)
            load_v(0, 4)
            load_x(6, 0)
            load_x(7, 1)
            load_xr(0, 4)
            load_xr(0, 5)
            for s in range(1, STEPS):
                if s in (2, 4, 5):
                    load_v(0, {2: 5, 4: 6, 5: 7}[s])
                store_parts(s)
                if s + 1 < STEPS:
                    split_step(s + 1)
            load_x(8, 0)
            load_x(9, 1)
            for slot in range(2):
                sp.wait_ge(w_stored[slot], 16 * STEPS // 2)
            load_parts(0, 0, groups_through_0(STEPS - 2))
            for T in range(HT, TILES):
                store_x2(0, T)
                if T + 2 < TILES:
                    load_xr(0, T + 2)
            load_parts(1, 1, groups_through_0(STEPS - 1))
            for T in range(TILES + 2, 2 * TILES):
                load_x(T, T % 2)
            load_v(1, 0)
            load_xr(1, 0)
            load_xr(1, 1)
            for s in range(2, STEPS):
                load_parts(s, s % 2, groups_through_0(STEPS + s - 2))
                if s in (2, 4, 5, 7):
                    load_v(1, {2: 1, 4: 2, 5: 3, 7: 4}[s])
            split_step(STEPS)

            def store_out(b, s):
                sp.wait_ge(out_added, 2 * CB * b + 2 * (s + 1))
                sp.dma_start(out[b, s], xo[:, s % 2, :, :]).then_inc(out_stored[s % 2], 16)

            def second_product(b, pairs, split=False, front=True, more=True):
                for s in range(STEPS):
                    if s in pairs:
                        load_v(b + 1, pairs[s])
                    if split:
                        store_parts(STEPS + s)
                    if split and s + 1 < STEPS:
                        split_step(STEPS + s + 1)
                    if not split and s + 1 < STEPS:
                        load_parts(STEPS + s + 1, (s + 1) % 2, groups_through(b, STEPS + s - 1))
                    if s + 1 == STEPS and more:
                        if split:
                            for slot in range(2):
                                sp.wait_ge(w_stored[slot], 16 * STEPS)
                        load_parts(0, 0, groups_through(b, 2 * STEPS - 2))
                    if not (isinstance(b, int) and b == 0 and s < 2):
                        sp.wait_ge(out_stored[s % 2], 64 * b + 16 * (s // 2))
                    if s == 0:
                        for i in range(2):
                            sp.wait_ge(x2_stored[i], 64 * (b + 1))
                    sp.dma_start(xo[:, s % 2, :, :], x2_dram[b, s]).then_inc(xo_landed[s % 2], 16)
                    if front:
                        store_x2(b + 1, s)
                        if s + 2 < TILES:
                            load_xr(b + 1, s + 2)
                    if s >= 1:
                        store_out(b, s - 1)

            second_product(0, {0: 5, 1: 6, 2: 7}, split=True)

            def first_product(b, front=True):
                nb = b + 1

                def step(s, j):
                    load_parts(s + 1, (j + 1) % 2, GROUPS * b + 2 * Q * s)

                for s in range(HT):
                    step(s, s % 2)
                    if front:
                        load_x(TILES * nb + 2 * s, 0)
                        load_x(TILES * nb + 2 * s + 1, 1)
                        if s >= 1:
                            load_v(nb, s - 1)
                    if s == 0:
                        store_out(b - 1, STEPS - 1)
                if front:
                    load_xr(nb, 0)
                    load_xr(nb, 1)
                with sp.Fori(HT // 2, STEPS // 2) as p:
                    for j in range(2):
                        step(2 * p + j, j)
                        if front:
                            load_v(nb, 2 * p + j - 1)

            with sp.Fori(1, B - 1) as b:
                first_product(b)
                second_product(b, {0: 7})
            first_product(B - 1, front=False)
            second_product(B - 1, {}, front=False, more=False)
            store_out(B - 1, STEPS - 1)
            for slot in range(2):
                sp.wait_ge(out_stored[slot], 64 * B)

        @block.gpsimd
        def _(pool):
            nc.gpsimd.memset(ident[:, :], 0.0).then_inc(s_pool0, 1)
            nc.gpsimd.memset(power[:, :], -0.5).then_inc(s_pool0, 1)
            nc.gpsimd.memset(st_o[:, :], NEG_INF).then_inc(s_pool0, 1)
            nc.gpsimd.memset(st_pq[:, :, :], 0.0).then_inc(s_pool0, 1)
            pool.wait_ge(s_pool0, 4)
            nc.gpsimd.affine_select(out=ident[:, :], in_=ident[:, :], compare_op=ALU.not_equal, fill=1.0,
                                    base=0, pattern=[[-1, P]], channel_multiplier=1).then_inc(s_pool0, 1)
            pool.wait_ge(s_pool0, 5)
            nc.gpsimd.tensor_copy(ident16[:, :], ident[:, :]).then_inc(s_pool0, 1)

            def rstd_of(i, T):
                pool.wait_ge(ve_done[i], T + 1)
                nc.gpsimd.tensor_tensor(rstd[:, i, 1:2], rstd[:, i, 0:1], power[:, :], ALU.pow)\
                    .then_inc(rstd_done[i], 1)

            def products(b, pair):
                for j in range(2):
                    n = UNITS * b + 2 * pair + j
                    pool.wait_ge(e2_done, n + 1)
                    pool.wait_ge(v_landed[j], 16 * (CB * b + pair + 1))
                    pool.wait_ge(d2_done, n + 1)
                    pool.wait_ge(z_raw, n + 1)
                    pool.wait_ge(o_saved, n + 1)
                    nc.gpsimd.tensor_tensor(uOE[:, j, 0, 1:], uOE[:, j, 1, 1:], uV[:, j, :], ALU.mult)\
                        .then_inc(ev_done, 1)
                for j in range(2):
                    n = UNITS * b + 2 * pair + j
                    pool.wait_ge(r_done, n + 1)
                    pool.wait_ge(ev_done, n + 1)
                    nc.gpsimd.tensor_tensor(uV[:, j, :], uR[:, j, :], uV[:, j, :], ALU.mult)\
                        .then_inc(rv_done, 1)

            def lo_piece(g):
                pool.wait_ge(ws_done, g + 1)
                nc.gpsimd.tensor_tensor(W[:, (g // Q) % 2, 1, g % Q, :], stage[:, g % 2, :],
                                        W[:, (g // Q) % 2, 0, g % Q, :], ALU.subtract).then_inc(lo_done, 1)

            for T in range(HT):
                rstd_of(0, T)
            products(0, 0)
            for g in (0, 1):
                lo_piece(g)
            products(0, 1)
            for g in (2, 3, 4):
                lo_piece(g)
            products(0, 2)
            for g in (5, 6):
                lo_piece(g)
            products(0, 3)
            lo_piece(7)
            for T in range(HT):
                rstd_of(1, T)
            for T in range(HT, TILES):
                rstd_of(0, T)
            for s in range(STEPS):
                for q in range(Q):
                    if 1 <= s < STEPS - 1:
                        lo_piece(Q * (s + 1) + q)
                    if (s, q) in FRONT_P1:
                        products(0, FRONT_P1[s, q])
            for T in range(HT, TILES):
                rstd_of(1, T)
            for T in range(TILES, 2 * TILES):
                rstd_of(0, T)
            for pair in range(5):
                products(1, pair)
            for q in range(Q):
                lo_piece(NB + q)
            for s in range(STEPS):
                rstd_of(1, TILES + s)
                if s in FRONT_M0:
                    products(1, FRONT_M0[s])
                if s + 1 < STEPS:
                    for q in range(Q):
                        lo_piece(NB + Q * (s + 1) + q)
            with pool.Fori(1, B - 1) as b:
                for s in range(HT):
                    rstd_of(0, TILES * (b + 1) + 2 * s)
                    rstd_of(0, TILES * (b + 1) + 2 * s + 1)
                    if s >= 1:
                        products(b + 1, s - 1)
                with pool.Fori(HT - 1, CB - 1) as pair:
                    products(b + 1, pair)
                rstd_of(1, TILES * (b + 1))
                products(b + 1, CB - 1)
                with pool.Fori(1, TILES) as t:
                    rstd_of(1, TILES * (b + 1) + t)

        @block.scalar
        def _(act):
            act.wait_ge(s_const, 16 * 8)
            nc.scalar.activation(tg[:, :], gates[:, :], ACT.Tanh).then_inc(s_tg, 1)

            def copy_k(b, tile, first=False):
                act.wait_ge(kt_done, TILES * b + tile + 1)
                if not first:
                    act.wait_ge(yt_done, TILES * (b - 1) + (TILES if isinstance(tile, int) and tile >= HT else HT))
                h = tile // HT
                nc.scalar.activation(K[:, CB * h:CB * (h + 1), P * (tile % HT):P * (tile % HT + 1)],
                                     trA[:, :, :], ACT.Copy).then_inc(k_copied, 1)

            def copy_xt(b, tile):
                act.wait_ge(xt_done, TILES * b + tile + 1)
                nc.scalar.activation(XT[:, :, P * tile:P * (tile + 1)], trX[:, :, :], ACT.Copy)\
                    .then_inc(xt_copied, 1)

            def exps(b, pair):
                n = UNITS * b + 2 * pair
                for j in range(2):
                    act.wait_ge(d1_done, n + j + 1)
                    nc.scalar.activation(uOE[:, j, 1, 1:], uOE[:, j, 1, 1:], ACT.Exp).then_inc(e2_done, 1)
                for j in range(2):
                    act.wait_ge(d2_done, n + j + 1)
                    nc.scalar.activation(uA[:, j, :], uA[:, j, :], ACT.Exp).then_inc(a2_done, 1)
                for j in range(2):
                    act.wait_ge(z_done, n + j + 1)
                    nc.scalar.activation(uR[:, j, :], uR[:, j, :], ACT.Exp).then_inc(r_done, 1)

            def hi_piece(g):
                s = g // Q
                v = s if s < STEPS else s + STEPS
                act.wait_ge(wst_landed[g % 2], 16 * (g // 2 + 1))
                if g % Q == 0 and v >= 2:
                    act.wait_ge(mm_done, groups_through_0(v - 2))
                    act.wait_ge(w_stored[s % 2], 16 * (s // 2))
                nc.scalar.activation(W[:, s % 2, 0, g % Q, :], stage[:, g % 2, :], ACT.Copy, scale=W_SCALE)\
                    .then_inc(hi_done, 1)
                act.wait_ge(hi_done, g + 1)
                nc.scalar.activation(stage[:, g % 2, :], stage[:, g % 2, :], ACT.Copy, scale=W_SCALE)\
                    .then_inc(ws_done, 1)

            def gelu(m, nb, half, bank):
                act.wait_ge(mm_done, m + 1)
                nc.scalar.activation(DT[:, nb, HALF * half:HALF * (half + 1)], acc[bank][:, :], ACT.Gelu,
                                     bias=b0[:, bass.ds(nb, 1)], scale=1.0 / W_SCALE).then_inc(acc_drained, 1)

            def round_e(b, s, half):
                act.wait_ge(mm_done, GROUPS * b + GROUPS1 + 2 * s + half + 1)
                if not (isinstance(b, int) and b == 0 and s == 0):
                    act.wait_ge(et_done, 2 * CB * b + 2 * s + half - 1)
                nc.scalar.activation(e16[:, half, :], acc[(2 * s + half) % BANKS][:, :], ACT.Identity,
                                     bias=b1[:, s:s + 1], scale=1.0 / W_SCALE).then_inc(acc_drained, 1)

            for T in range(HT):
                copy_k(0, T, first=True)
            exps(0, 0)
            for g in (0, 1):
                hi_piece(g)
            exps(0, 1)
            for g in (2, 3, 4):
                hi_piece(g)
            exps(0, 2)
            for g in (5, 6):
                hi_piece(g)
            exps(0, 3)
            hi_piece(7)
            for T in range(HT):
                copy_xt(0, T)
            for s in range(STEPS):
                for q in range(Q):
                    if s == 0:
                        copy_k(0, HT + q, first=True)
                    gelu(Q * s + q, Q * s + q, 0, q)
                    if 1 <= s < STEPS - 1:
                        hi_piece(Q * (s + 1) + q)
                    if (s, q) in FRONT_P1:
                        exps(0, FRONT_P1[s, q])
            for T in range(HT, TILES):
                copy_xt(0, T)
            for s in range(STEPS):
                for q in range(Q):
                    gelu(NB + Q * s + q, Q * s + q, 1, q)
                    if s < 2:
                        copy_k(1, Q * s + q)
                    if (s, q) in FRONT_P2:
                        exps(1, FRONT_P2[s, q])
                    if s == STEPS - 1:
                        hi_piece(NB + q)

            def second_product(b, pairs, split=False, front=True):
                for s in range(STEPS):
                    if s in pairs:
                        exps(b + 1, pairs[s])
                    if split and s + 1 < STEPS:
                        hi_piece(NB + Q * (s + 1))
                        hi_piece(NB + Q * (s + 1) + 1)
                    round_e(b, s, 0)
                    if front:
                        copy_xt(b + 1, s)
                    if split and s + 1 < STEPS:
                        hi_piece(NB + Q * (s + 1) + 2)
                        hi_piece(NB + Q * (s + 1) + 3)
                    round_e(b, s, 1)

            second_product(0, FRONT_M0, split=True)

            def first_product(b, front=True):
                def step(s, tiles, pair):
                    for q in range(Q):
                        for half in range(2):
                            i = 2 * q + half
                            gelu(GROUPS * b + 2 * Q * s + i, Q * s + q, half, i % BANKS)
                            if i in (1, 2) and tiles is not None:
                                copy_k(b + 1, tiles + i - 1)
                            if i == 3 and pair is not None:
                                exps(b + 1, pair)

                for s in range(HT):
                    step(s, 2 * s if front else None, s - 1 if front and s else None)
                with act.Fori(HT, STEPS) as s:
                    step(s, None, s - 1 if front else None)

            with act.Fori(1, B - 1) as b:
                first_product(b)
                second_product(b, {0: CB - 1})
            first_product(B - 1, front=False)
            second_product(B - 1, {}, front=False)

        @block.vector
        def _(dve):
            def norm_stats(i, b, tile, src, normalised):
                T = TILES * b + tile
                first = isinstance(T, int) and T == 0
                if not first:
                    dve.wait_ge(normalised, T)
                    dve.wait_ge(mv_done[i], T)
                both = 2 * T + 2 if isinstance(T, int) else dve.to_reg(2 * T + 2)
                for h in range(2):
                    nc.vector.bn_stats(stats[:, i, h, :], src[:, 512 * h:512 * (h + 1)]).then_inc(bn_done[i], 1)
                dve.wait_ge(s_pool0, 6)
                dve.wait_ge(bn_done[i], both)
                nc.vector.bn_aggr(mv[:, i, :], stats[:, i, :, :].rearrange("p h k -> p (h k)"))\
                    .then_inc(mv_done[i], 1)
                dve.wait_ge(mv_done[i], T + 1)
                nc.vector.tensor_scalar(rstd[:, i, 0:1], mv[:, i, 1:2], EPS, None, ALU.add).then_inc(ve_done[i], 1)

            def normalise(i, b, tile, out, src, sem):
                dve.wait_ge(rstd_done[i], TILES * b + tile + 1)
                nc.vector.tensor_scalar(out, src, mv[:, i, 0:1], rstd[:, i, 1:2], ALU.subtract, ALU.mult)\
                    .then_inc(sem, 1)

            def norm_k(b, tile):
                slot = tile % 2
                dve.wait_ge(x_landed[slot], 16 * (HT * b + tile // 2 + 1))
                norm_stats(0, b, tile, xin[:, slot, :], xn_ready)
                normalise(0, b, tile, xin[:, slot, :], xin[:, slot, :], xn_ready)

            def residual(b, tile):
                slot = tile % 2
                dve.wait_ge(yt_done, TILES * b + tile + 1)
                dve.wait_ge(xr_landed[slot], 16 * (HT * b + tile // 2 + 1))
                nc.vector.scalar_tensor_tensor(
                    xres[:, slot, :], trA[:, :, :].rearrange("p c h -> p (c h)"), tg[:, 0:1],
                    xres[:, slot, :], ALU.mult, ALU.add).then_inc(x2_done, 1)
                dve.wait_ge(x2_done, TILES * b + tile + 1)
                norm_stats(1, b, tile, xres[:, slot, :], xh_ready)

            def norm_x2(b, tile):
                if not (isinstance(b, int) and b == 0 and tile == 0):
                    dve.wait_ge(xt_done, TILES * b + tile)
                normalise(1, b, tile, xh[:, :], xres[:, tile % 2, :], xh_ready)

            def units(b, pair):
                n = UNITS * b + 2 * pair
                first = isinstance(n, int) and n == 0
                u = [2 * pair + j for j in range(2)]
                k = [K[:, u[j], :] for j in range(2)]
                before = [[uOE[:, j, i, 0:HALF] for i in range(2)] for j in range(2)]
                now = [[uOE[:, j, i, 1:] for i in range(2)] for j in range(2)]
                for j in range(2):
                    if not first:
                        dve.wait_ge(y_done, n + j - 1)
                        dve.wait_ge(o_saved, n + j - 1)
                    nc.vector.tensor_copy(uOE[:, j, 0, 0:1], st_o[:, bass.ds(u[j], 1)]).then_inc(o_seeded, 1)
                for j in range(2):
                    nc.vector.tensor_tensor_scan(now[j][0], w_u[:, 0, bass.ds(u[j], 1)].to_broadcast([P, HALF]),
                                                 k[j], st_o[:, bass.ds(u[j], 1)], ALU.add, ALU.max)\
                        .then_inc(o_scanned, 1)
                for j in range(2):
                    dve.wait_ge(o_scanned, n + j + 1)
                    nc.vector.tensor_tensor(now[j][1], k[j], now[j][0], ALU.subtract).then_inc(d1_done, 1)
                for j in range(2):
                    dve.wait_ge(o_seeded, n + j + 1)
                    nc.vector.scalar_tensor_tensor(uA[:, j, :], before[j][0], w_u[:, 0, bass.ds(u[j], 1)],
                                                   now[j][0], ALU.add, ALU.subtract).then_inc(d2_done, 1)
                for j in range(2):
                    nc.vector.scalar_tensor_tensor(uR[:, j, :], k[j], w_u[:, 1, bass.ds(u[j], 1)],
                                                   before[j][0], ALU.add, ALU.subtract).then_inc(z_raw, 1)
                for j in range(2):
                    nc.vector.tensor_copy(st_o[:, bass.ds(u[j] + CB, 1)], uOE[:, j, 0, HALF:]).then_inc(o_saved, 1)
                for j in range(2):
                    dve.wait_ge(z_raw, n + j + 1)
                    nc.vector.tensor_scalar(uR[:, j, :], uR[:, j, :], R_CAP, None, ALU.min).then_inc(z_done, 1)
                for j in range(2):
                    dve.wait_ge(d2_done, n + j + 1)
                    if not first:
                        dve.wait_ge(pq_saved, n + j - 1)
                    nc.vector.tensor_copy(uOE[:, j, :, 0], st_pq[:, u[j], :]).then_inc(pq_seeded, 1)
                for j in range(2):
                    dve.wait_ge(a2_done, n + j + 1)
                    dve.wait_ge(ev_done, n + j + 1)
                    nc.vector.tensor_tensor_scan(now[j][1], uA[:, j, :], now[j][1],
                                                 st_pq[:, u[j], 1:2], ALU.mult, ALU.add).then_inc(q_scanned, 1)
                for j in range(2):
                    nc.vector.tensor_tensor_scan(now[j][0], uA[:, j, :], now[j][0],
                                                 st_pq[:, u[j], 0:1], ALU.mult, ALU.add).then_inc(p_scanned, 1)
                for j in range(2):
                    dve.wait_ge(rv_done, n + j + 1)
                    dve.wait_ge(pq_seeded, n + j + 1)
                    dve.wait_ge(q_scanned, n + j + 1)
                    nc.vector.tensor_tensor(uR[:, j, :], uR[:, j, :], before[j][1], ALU.add).then_inc(den_done, 1)
                for j in range(2):
                    dve.wait_ge(p_scanned, n + j + 1)
                    nc.vector.tensor_tensor(uV[:, j, :], uV[:, j, :], before[j][0], ALU.add).then_inc(num_done, 1)
                for j in range(2):
                    nc.vector.tensor_copy(st_pq[:, u[j] + CB, :], uOE[:, j, :, HALF]).then_inc(pq_saved, 1)
                for j in range(2):
                    dve.wait_ge(den_done, n + j + 1)
                    nc.vector.reciprocal(uR[:, j, :], uR[:, j, :]).then_inc(rec_done, 1)
                for j in range(2):
                    dve.wait_ge(rec_done, n + j + 1)
                    dve.wait_ge(num_done, n + j + 1)
                    nc.vector.tensor_tensor(k[j], uV[:, j, :], uR[:, j, :], ALU.mult).then_inc(y_done, 1)

            def add_out(b, s, half):
                dve.wait_ge(et_done, 2 * CB * b + 2 * s + half + 1)
                dve.wait_ge(xo_landed[s % 2], 16 * (CB // 2 * b + s // 2 + 1))
                o = xo[:, s % 2, HT * half:HT * (half + 1), :].rearrange("p t h -> p (t h)")
                nc.vector.scalar_tensor_tensor(o, trE[:, :, :].rearrange("p t h -> p (t h)"), tg[:, 1:2], o,
                                               ALU.mult, ALU.add).then_inc(out_added, 1)

            def posts(b, tiles):
                for t in tiles:
                    residual(b, t)
                    norm_x2(b, t)

            for t in range(HT):
                norm_k(0, t)
            dve.wait_ge(s_const, 16 * 8)
            dve.wait_ge(s_pool0, 6)
            dve.wait_ge(k_copied, HT)
            for pair in range(HT):
                units(0, pair)
            dve.wait_ge(s_tg, 1)
            posts(0, range(HT))
            for t in range(HT, TILES):
                norm_k(0, t)
            dve.wait_ge(k_copied, TILES)
            for pair in range(HT, 2 * HT):
                units(0, pair)
            posts(0, range(HT, TILES))
            for t in range(TILES):
                norm_k(1, t)
            dve.wait_ge(k_copied, 2 * TILES)
            for pair in range(5):
                units(1, pair)

            def second_product(b, pairs, front=True):
                for s in range(STEPS):
                    if front:
                        residual(b + 1, s)
                    if s >= 1:
                        add_out(b, s - 1, 1)
                    if front:
                        norm_x2(b + 1, s)
                    if s in pairs:
                        units(b + 1, pairs[s])
                    add_out(b, s, 0)

            second_product(0, FRONT_M0)

            def first_product(b, front=True):
                if not front:
                    add_out(b - 1, STEPS - 1, 1)
                    return
                for s in range(HT):
                    norm_k(b + 1, 2 * s)
                    if s == 0:
                        add_out(b - 1, STEPS - 1, 1)
                    norm_k(b + 1, 2 * s + 1)
                    if s >= 1:
                        if s == 1:
                            dve.wait_ge(k_copied, TILES * (b + 1) + HT)
                        units(b + 1, s - 1)
                with dve.Fori(HT - 1, CB - 1) as pair:
                    dve.wait_ge(k_copied, TILES * (b + 2))
                    units(b + 1, pair)

            with dve.Fori(1, B - 1) as b:
                first_product(b)
                second_product(b, {0: CB - 1})
            first_product(B - 1, front=False)
            second_product(B - 1, {}, front=False)
            add_out(B - 1, STEPS - 1, 1)

        @block.tensor
        def _(pe):
            def transpose_k(b, tile, slot):
                T = TILES * b + tile
                pe.wait_ge(xn_ready, T + 1)
                if not (isinstance(T, int) and T == 0):
                    pe.wait_ge(k_copied, T)
                    if not (isinstance(b, int) and b == 0 and tile < HT):
                        pe.wait_ge(x2_done, HT if isinstance(b, int) and b == 0 else TILES * b)
                for c in range(CB):
                    mm = nc.tensor.transpose(trA[:, c, :], xin[:, slot, P * c:P * (c + 1)], ident[:, :])
                mm.then_inc(kt_done, 1)

            def transpose_y(b, tile):
                T = TILES * b + tile
                h = tile // HT
                pe.wait_ge(y_done, UNITS * b + CB * (h + 1))
                pe.wait_ge(k_copied, HT if isinstance(T, int) and T < HT else TILES * (b + 1))
                if not (isinstance(T, int) and T == 0):
                    pe.wait_ge(x2_done, T)
                for c in range(CB):
                    mm = nc.tensor.transpose(trA[:, c, :], K[:, CB * h + c, P * (tile % HT):P * (tile % HT + 1)],
                                             ident[:, :])
                mm.then_inc(yt_done, 1)

            def transpose_x2(b, tile):
                T = TILES * b + tile
                pe.wait_ge(xh_ready, T + 1)
                if not (isinstance(T, int) and T == 0):
                    pe.wait_ge(xt_copied, T)
                for c in range(CB):
                    mm = nc.tensor.transpose(trX[:, c, :], xh[:, P * c:P * (c + 1)], ident16[:, :])
                mm.then_inc(xt_done, 1)

            def transpose_e(b, s, half):
                n = 2 * CB * b + 2 * s + half
                pe.wait_ge(acc_drained, GROUPS * b + GROUPS1 + 2 * s + half + 1)
                if not (isinstance(n, int) and n == 0):
                    pe.wait_ge(out_added, n)
                for t in range(HT):
                    mm = nc.tensor.transpose(trE[:, t, :], e16[:, half, P * t:P * (t + 1)], ident16[:, :])
                mm.then_inc(et_done, 1)

            def group1(m, slot, q, half, bank):
                if not (isinstance(m, int) and m < BANKS):
                    pe.wait_ge(acc_drained, m - BANKS + 1)
                for c in range(CB):
                    for part in range(2):
                        mm = nc.tensor.matmul(acc[bank][:, :], W[:, slot, part, q, P * c:P * (c + 1)],
                                              XT[:, c, HALF * half:HALF * (half + 1)],
                                              start=(c == 0 and part == 0), stop=(c == CB - 1 and part == 1))
                mm.then_inc(mm_done, 1)

            def second_product(b, front=True):
                for s in range(STEPS):
                    slot = s % 2
                    split = isinstance(b, int) and b == 0
                    if not split:
                        pe.wait_ge(w_landed[slot], 16 * (Q + CB * (b - 1) + Q + s // 2 + 1))
                    for half in range(2):
                        m = GROUPS * b + GROUPS1 + 2 * s + half
                        bank = (2 * s + half) % BANKS
                        if front and half == 0:
                            transpose_y(b + 1, s)
                        pe.wait_ge(acc_drained, m - BANKS + 1)
                        if front and half == 1:
                            transpose_x2(b + 1, s)
                        for q in range(Q):
                            if split and half == 0:
                                pe.wait_ge(lo_done, NB + Q * s + q + 1)
                            if s == 0 and half == 0 and q == Q - 1:
                                pe.wait_ge(acc_drained, GROUPS * b + GROUPS1)
                            for c in range(CB):
                                nb = CB * q + c
                                for part in range(2):
                                    mm = nc.tensor.matmul(
                                        acc[bank][:, :], W[:, slot, part, q, P * c:P * (c + 1)],
                                        DT[:, nb, HALF * half:HALF * (half + 1)],
                                        start=(nb == 0 and part == 0), stop=(nb == NB - 1 and part == 1))
                            if q == 0 and (s, half) != (0, 0):
                                transpose_e(b, *((s, 0) if half else (s - 1, 1)))
                        mm.then_inc(mm_done, 1)

            pe.wait_ge(s_pool0, 6)
            for t in range(HT):
                transpose_k(0, t, t % 2)
            posts = [("y", 0), ("y", 1), ("x", 0), ("y", 2), ("x", 1), ("y", 3), ("x", 2), ("x", 3)]
            for what, t in posts:
                (transpose_y if what == "y" else transpose_x2)(0, t)
            pe.wait_ge(xt_copied, HT)
            for s in range(2):
                for q in range(Q):
                    pe.wait_ge(lo_done, Q * s + q + 1)
                    group1(Q * s + q, s, q, 0, q)
                    if s == 0:
                        transpose_k(0, HT + q, q % 2)
            with pe.Fori(1, STEPS // 2) as p:
                for slot in range(2):
                    for q in range(Q):
                        m = 2 * Q * p + Q * slot + q
                        pe.wait_ge(lo_done, m + 1)
                        group1(m, slot, q, 0, q)
            for what, t in posts:
                (transpose_y if what == "y" else transpose_x2)(0, HT + t)
            pe.wait_ge(xt_copied, TILES)
            for s in range(2):
                pe.wait_ge(w_landed[s], 16)
                for q in range(Q):
                    group1(NB + Q * s + q, s, q, 1, q)
                    transpose_k(1, Q * s + q, q % 2)
            with pe.Fori(1, STEPS // 2) as p:
                for slot in range(2):
                    pe.wait_ge(w_landed[slot], 16 * p + 16)
                    for q in range(Q):
                        group1(NB + 2 * Q * p + Q * slot + q, slot, q, 1, q)
            second_product(0)

            def first_product(b, front=True):
                pe.wait_ge(xt_copied, TILES * (b + 1))

                def pair_of_steps(p, tiles, pending=False):
                    for slot in range(2):
                        pe.wait_ge(w_landed[slot], 16 * (Q + CB * (b - 1) + p + 1))
                        for i in range(2 * Q):
                            m = GROUPS * b + 4 * Q * p + 2 * Q * slot + i
                            group1(m, slot, i // 2, i % 2, i % BANKS)
                            if pending and slot == 0 and i == 0:
                                transpose_e(b - 1, STEPS - 1, 1)
                            if tiles and i in (1, 2):
                                transpose_k(b + 1, 4 * p + 2 * slot + i - 1, i - 1)

                pair_of_steps(0, front, pending=True)
                pair_of_steps(1, front)
                with pe.Fori(2, STEPS // 2) as p:
                    pair_of_steps(p, False)

            with pe.Fori(1, B - 1) as b:
                first_product(b)
                second_product(b)
            first_product(B - 1, front=False)
            second_product(B - 1, front=False)
            transpose_e(B - 1, STEPS - 1, 1)


FRONT_P1 = {(0, 3): 4, (2, 1): 5, (3, 3): 6, (5, 0): 7}
FRONT_P2 = {(1, 3): 0, (3, 0): 1, (4, 2): 2, (6, 0): 3, (7, 2): 4}
FRONT_M0 = {0: 5, 1: 6, 2: 7}


def kernel(x, ctx_2048, g_xattn, g_ffn, L0_xattn_w, L0_xattn_u, L0_ffn_W0, L0_ffn_bias0, L0_ffn_W1,
           L0_ffn_bias1):
    import concourse.bacc as bacc
    from concourse.bass_utils import run_bass_kernel_spmd

    def blocks(v, n):
        return np.asarray(v).reshape(n, P).T

    arrays = {
        "x": np.asarray(x).reshape(B * TILES, P, H),
        "vT": np.asarray(ctx_2048).reshape(B, 2, HALF, CB, P).transpose(0, 1, 3, 4, 2).reshape(B, UNITS, P, HALF),
        "g_xattn": np.broadcast_to(np.asarray(g_xattn).reshape(1, 1), (P, 1)),
        "g_ffn": np.broadcast_to(np.asarray(g_ffn).reshape(1, 1), (P, 1)),
        "w": blocks(L0_xattn_w, CB),
        "u": blocks(L0_xattn_u, CB),
        "w0": np.asarray(L0_ffn_W0).reshape(NB, P, CB, P).transpose(0, 3, 2, 1).reshape(NB, P, 1024),
        "bias0": blocks(L0_ffn_bias0, NB),
        "w1": np.asarray(L0_ffn_W1).reshape(CB, P, Q, CB, P).transpose(0, 2, 4, 3, 1).reshape(NB, P, 1024),
        "bias1": blocks(L0_ffn_bias1, CB),
    }
    arrays = {n: np.ascontiguousarray(a) for n, a in arrays.items()}
    nc = bacc.Bacc("TRN2", target_bir_lowering=False, num_devices=1)
    args = {n: nc.dram_tensor(f"{n}_in", a.shape, mybir.dt.from_np(a.dtype), kind="ExternalInput").ap()
            for n, a in arrays.items()}
    out = nc.dram_tensor("out", (B, CB, P, TILES, P), F32, kind="ExternalOutput").ap()
    build(nc, **args, out=out)
    r = run_bass_kernel_spmd(nc, [{f"{n}_in": a for n, a in arrays.items()}], core_ids=[0])
    return r.results[0]["out"].transpose(0, 3, 2, 1, 4).reshape(B, L, H)
```

```python
from contextlib import ExitStack

import numpy as np
import concourse.bass as bass
from concourse import mybir

ALU = mybir.AluOpType
ACT = mybir.ActivationFunctionType
F32 = mybir.dt.float32
F16 = mybir.dt.float16

P = 128
B, L, H, N = 4, 1024, 1024, 4096
CB = H // P
TILES = L // P
HALF = 512
HT = HALF // P
UNITS = 2 * CB
NB = N // P
Q = 4
STEPS = NB // Q
assert STEPS == CB == 8 and TILES == 8
GROUPS1 = 2 * NB
GROUPS = GROUPS1 + 2 * CB
BANKS = 4
EPS = 1e-5
NEG_INF = -1e38
R_CAP = 60.0
W_SCALE = 1024.0


def groups_through(b, step):
    if step < STEPS:
        return GROUPS * b + 2 * Q * (step + 1)
    return GROUPS * b + GROUPS1 + 2 * (step - STEPS + 1)


def groups_through_0(v):
    if v < 2 * STEPS:
        return Q * (v + 1)
    return GROUPS1 + 2 * (v - 2 * STEPS + 1)


def build(nc, x, vT, g_xattn, g_ffn, w, u, w0, bias0, w1, bias1, out):
    x2_dram = nc.dram_tensor("x2_dram", (B, CB, P, TILES, P), F32).ap()
    parts_dram = nc.dram_tensor("parts_dram", (2 * STEPS, P, 2 * Q * 1024), F16).ap()
    x2_view = x2_dram.rearrange("b c p t h -> b t p c h")

    with ExitStack() as ctx:
        def sb(name, shape, dt=F32):
            return ctx.enter_context(nc.sbuf_tensor(name, shape, dt))

        def ps(name, shape, dt=F32):
            return ctx.enter_context(nc.psum_tensor(name, shape, dt))

        def sem(name):
            return ctx.enter_context(nc.semaphore(name))

        def sems(name, n=2):
            return [sem(f"{name}{i}") for i in range(n)]

        ident = sb("ident", [P, P])
        ident16 = sb("ident16", [P, P], F16)
        gates = sb("gates", [P, 2])
        tg = sb("tg", [P, 2])
        power = sb("power", [P, 1])
        w_u = sb("w_u", [P, 2, UNITS])
        b0 = sb("b0", [P, NB])
        b1 = sb("b1", [P, CB])
        xin = sb("xin", [P, 2, H])
        xres = sb("xres", [P, 2, H])
        xh = sb("xh", [P, H], F16)
        stats = sb("stats", [P, 2, 2, 6])
        mv = sb("mv", [P, 2, 2])
        rstd = sb("rstd", [P, 2, 2])
        K = sb("K", [P, UNITS, HALF])
        uV = sb("uV", [P, 2, HALF])
        uOE = sb("uOE", [P, 2, 2, HALF + 1])
        uA = sb("uA", [P, 2, HALF])
        uR = sb("uR", [P, 2, HALF])
        st_o = sb("st_o", [P, UNITS + CB])
        st_pq = sb("st_pq", [P, UNITS + CB, 2])
        XT = sb("XT", [P, CB, L], F16)
        DT = sb("DT", [P, NB, L], F16)
        stage = sb("stage", [P, 3, 1024])
        W = sb("W", [P, 2, 2, Q, 1024], F16)
        e16 = sb("e16", [P, 2, HALF], F16)
        xo = sb("xo", [P, 2, TILES, P])

        rings = [[stage[:, i, :] for i in range(3)] + [xo[:, i, :, :].rearrange("p t h -> p (t h)") for i in range(2)],
                 [stage[:, i, :] for i in range(3)]]

        def ring_slot(g):
            before = [k % 5 if k < NB else k % 3 for k in range(g)]
            slot = g % 5 if g < NB else g % 3
            return slot, before.count(slot)

        def x_tile(T, slot):
            return xres[:, slot, :] if isinstance(T, int) and 2 <= T < HT else xin[:, slot, :]

        acc = [ps(f"acc{i}", [P, HALF]) for i in range(BANKS)]
        trA = ps("trA", [P, CB, P])
        trX = ps("trX", [P, CB, P], F16)
        trE = ps("trE", [P, HT, P], F16)

        s_const = sem("const_landed")
        s_tg = sem("tg_ready")
        s_pool0 = sem("pool_constants")
        x_landed, xr_landed, v_landed = sems("x_landed"), sems("xr_landed"), sems("v_landed")
        x2_stored, xo_landed, out_stored = sems("x2_stored"), sems("xo_landed"), sems("out_stored")
        wst_landed, w_landed, w_stored = sems("wst_landed", 5), sems("w_landed"), sems("w_stored")
        bn_done, mv_done, ve_done, rstd_done = (sems(n) for n in ("bn_done", "mv_done", "ve_done", "rstd_done"))
        xn_ready, kt_done, k_copied = sem("xn_ready"), sem("kt_done"), sem("k_copied")
        yt_done, x2_done, xh_ready = sem("yt_done"), sem("x2_done"), sem("xh_ready")
        xt_done, xt_copied = sem("xt_done"), sem("xt_copied")
        o_seeded, o_scanned, o_saved = sem("o_seeded"), sem("o_scanned"), sem("o_saved")
        d1_done, d2_done, z_raw, z_done = sem("d1_done"), sem("d2_done"), sem("z_raw"), sem("z_done")
        e2_done, a2_done, r_done = sem("e2_done"), sem("a2_done"), sem("r_done")
        ev_done, rv_done = sem("ev_done"), sem("rv_done")
        pq_seeded, q_scanned, p_scanned, pq_saved = (sem(n) for n in ("pq_seeded", "q_scanned", "p_scanned", "pq_saved"))
        den_done, num_done, rec_done, y_done = sem("den_done"), sem("num_done"), sem("rec_done"), sem("y_done")
        hi_done, ws_done, lo_done = sem("hi_done"), sem("ws_done"), sem("lo_done")
        mm_done, acc_drained = sem("mm_done"), sem("acc_drained")
        et_done, out_added = sem("et_done"), sem("out_added")

        block = ctx.enter_context(nc.Block())

        @block.sync
        def _(sp):
            def load_x(T, slot):
                if isinstance(T, int) and 2 <= T < HT:
                    sp.dma_start(x_tile(T, slot), x[T]).then_inc(xr_landed[slot], 16)
                    return
                if not (isinstance(T, int) and T < 2):
                    sp.wait_ge(kt_done, T - HT + 1 if isinstance(T, int) and T < HT + 2 else T - 1)
                sp.dma_start(x_tile(T, slot), x[T]).then_inc(x_landed[slot], 16)

            def load_xr(b, tile):
                slot, T = tile % 2, TILES * b + tile
                if isinstance(T, int) and T < 2:
                    sp.wait_ge(kt_done, T + 3)
                else:
                    sp.wait_ge(x2_stored[slot], 64 * b + 16 * (tile // 2))
                    sp.wait_ge(xh_ready, T - 1)
                sp.dma_start(xres[:, slot, :], x[T]).then_inc(xr_landed[slot], 16)

            def store_x2(b, tile):
                sp.wait_ge(x2_done, TILES * b + tile + 1)
                sp.dma_start(x2_view[b, tile], xres[:, tile % 2, :].rearrange("p (c h) -> p c h", c=CB))\
                    .then_inc(x2_stored[tile % 2], 16)

            def load_v(b, pair):
                for j in range(2):
                    if not (isinstance(b, int) and isinstance(pair, int) and b == 0 and pair == 0):
                        sp.wait_ge(y_done, UNITS * b + 2 * pair + j - 1)
                    sp.dma_start(uV[:, j, :], vT[b, 2 * pair + j]).then_inc(v_landed[j], 16)

            def load_piece(g):
                slot, n = ring_slot(g)
                if n:
                    last = g - 5 if g < NB else g - 3
                    sp.wait_ge(lo_done, NB if last < NB <= g else last + 1)
                src = w0[g] if g < NB else w1[g - NB]
                sp.dma_start(rings[g // NB][slot], src).then_inc(wst_landed[slot], 16)

            def store_piece(g):
                s = g // Q
                sp.wait_ge(lo_done, g + 1)
                sp.dma_start(parts_dram[s].rearrange("p (a q n) -> p a q n", a=2, q=Q)[:, :, g % Q, :],
                             W[:, s % 2, :, g % Q, :]).then_inc(w_stored[s % 2], 16)

            def turn_piece(g):
                ahead = 5 if g < NB else 3
                if g + ahead < (NB if g < NB else 2 * NB):
                    load_piece(g + ahead)
                store_piece(g)

            def load_parts(s, slot, groups):
                sp.wait_ge(mm_done, groups)
                sp.dma_start(W[:, slot, :, :, :].rearrange("p a q n -> p (a q n)"), parts_dram[s])\
                    .then_inc(w_landed[slot], 16)

            for T in range(HT):
                load_x(T, T % 2)
            load_v(0, 0)
            sp.dma_start(w_u[:, 0, 0:CB], w).then_inc(s_const, 16)
            sp.dma_start(w_u[:, 0, CB:UNITS], w).then_inc(s_const, 16)
            sp.dma_start(w_u[:, 1, 0:CB], u).then_inc(s_const, 16)
            sp.dma_start(w_u[:, 1, CB:UNITS], u).then_inc(s_const, 16)
            sp.dma_start(gates[:, 0:1], g_xattn).then_inc(s_const, 16)
            sp.dma_start(gates[:, 1:2], g_ffn).then_inc(s_const, 16)
            sp.dma_start(b0[:, :], bias0).then_inc(s_const, 16)
            sp.dma_start(b1[:, :], bias1).then_inc(s_const, 16)
            load_x(4, 0)
            load_x(5, 1)
            load_xr(0, 0)
            load_xr(0, 1)
            for g in range(5):
                load_piece(g)
            for item in ("v1", 0, 1, "v2", 2, 3, 4, "v3", 5, 6, 7):
                if isinstance(item, int):
                    turn_piece(item)
                else:
                    load_v(0, int(item[1]))
            for T in range(HT):
                store_x2(0, T)
                if T + 2 < HT:
                    load_xr(0, T + 2)
            load_v(0, 4)
            load_x(6, 0)
            load_x(7, 1)
            load_xr(0, 4)
            load_xr(0, 5)
            for g in range(2 * Q, NB):
                if g in V_P1:
                    load_v(0, V_P1[g])
                turn_piece(g)
            load_x(8, 0)
            load_x(9, 1)
            for slot in range(2):
                sp.wait_ge(w_stored[slot], 16 * NB // 2)
            load_parts(0, 0, groups_through_0(STEPS - 2))
            store_x2(0, HT)
            load_xr(0, HT + 2)
            store_x2(0, HT + 1)
            load_xr(0, HT + 3)
            load_parts(1, 1, groups_through_0(STEPS - 1))
            for T in range(HT + 2, TILES):
                store_x2(0, T)
            for T in range(TILES + 2, TILES + 6):
                load_x(T, T % 2)
            load_parts(2, 0, groups_through_0(STEPS))
            for T in range(TILES + 6, 2 * TILES):
                load_x(T, T % 2)
            load_xr(1, 0)
            load_xr(1, 1)
            load_v(1, 0)
            for s in range(3, STEPS):
                load_parts(s, s % 2, groups_through_0(STEPS + s - 2))
                if s == 3:
                    for g in range(NB, NB + 3):
                        load_piece(g)
                else:
                    load_v(1, s - 3)
            for g in range(NB, NB + Q):
                turn_piece(g)

            def store_out(b, s):
                sp.wait_ge(out_added, 2 * CB * b + 2 * (s + 1))
                sp.dma_start(out[b, s], xo[:, s % 2, :, :]).then_inc(out_stored[s % 2], 16)

            def second_product(b, pairs, split=False, front=True, more=True):
                for s in range(STEPS):
                    if s in pairs:
                        load_v(b + 1, pairs[s])
                    if not split and s + 1 < STEPS:
                        load_parts(STEPS + s + 1, (s + 1) % 2, groups_through(b, STEPS + s - 1))
                    if s + 1 == STEPS and more:
                        if split:
                            for slot in range(2):
                                sp.wait_ge(w_stored[slot], 16 * NB)
                        load_parts(0, 0, groups_through(b, 2 * STEPS - 2))
                    if not (isinstance(b, int) and b == 0 and s < 2):
                        sp.wait_ge(out_stored[s % 2], 64 * b + 16 * (s // 2))
                    if s == 0:
                        for i in range(2):
                            sp.wait_ge(x2_stored[i], 64 * (b + 1))
                    sp.dma_start(xo[:, s % 2, :, :], x2_dram[b, s]).then_inc(xo_landed[s % 2], 16)
                    if front:
                        store_x2(b + 1, s)
                        if s + 2 < TILES:
                            load_xr(b + 1, s + 2)
                    if split and s + 1 < STEPS:
                        for g in range(NB + Q * (s + 1), NB + Q * (s + 2)):
                            turn_piece(g)
                    if s >= 1:
                        store_out(b, s - 1)

            second_product(0, {s: FRONT_M0[s] for s in range(1, HT)}, split=True)

            def first_product(b, front=True):
                nb = b + 1

                def step(s, j):
                    load_parts(s + 1, (j + 1) % 2, GROUPS * b + 2 * Q * s)

                for s in range(HT):
                    if front:
                        load_x(TILES * nb + 2 * s, 0)
                        load_x(TILES * nb + 2 * s + 1, 1)
                    step(s, s % 2)
                    if front and s >= 1:
                        load_v(nb, s - 1)
                    if s == 0:
                        store_out(b - 1, STEPS - 1)
                if front:
                    load_xr(nb, 0)
                    load_xr(nb, 1)
                with sp.Fori(HT // 2, STEPS // 2) as p:
                    for j in range(2):
                        step(2 * p + j, j)
                        if front:
                            load_v(nb, 2 * p + j - 1)

            with sp.Fori(1, B - 1) as b:
                first_product(b)
                second_product(b, {0: 7})
            first_product(B - 1, front=False)
            second_product(B - 1, {}, front=False, more=False)
            store_out(B - 1, STEPS - 1)
            for slot in range(2):
                sp.wait_ge(out_stored[slot], 64 * B)

        @block.gpsimd
        def _(pool):
            nc.gpsimd.memset(ident[:, :], 0.0).then_inc(s_pool0, 1)
            nc.gpsimd.memset(power[:, :], -0.5).then_inc(s_pool0, 1)
            nc.gpsimd.memset(st_o[:, :], NEG_INF).then_inc(s_pool0, 1)
            nc.gpsimd.memset(st_pq[:, :, :], 0.0).then_inc(s_pool0, 1)
            pool.wait_ge(s_pool0, 4)
            nc.gpsimd.affine_select(out=ident[:, :], in_=ident[:, :], compare_op=ALU.not_equal, fill=1.0,
                                    base=0, pattern=[[-1, P]], channel_multiplier=1).then_inc(s_pool0, 1)
            pool.wait_ge(s_pool0, 5)
            nc.gpsimd.tensor_copy(ident16[:, :], ident[:, :]).then_inc(s_pool0, 1)

            def rstd_of(i, T):
                pool.wait_ge(ve_done[i], T + 1)
                nc.gpsimd.tensor_tensor(rstd[:, i, 1:2], rstd[:, i, 0:1], power[:, :], ALU.pow)\
                    .then_inc(rstd_done[i], 1)

            def products(b, pair):
                before = [[uOE[:, j, i, 0:HALF] for i in range(2)] for j in range(2)]
                for j in range(2):
                    n = UNITS * b + 2 * pair + j
                    pool.wait_ge(e2_done, n + 1)
                    pool.wait_ge(v_landed[j], 16 * (CB * b + pair + 1))
                    pool.wait_ge(d2_done, n + 1)
                    pool.wait_ge(z_raw, n + 1)
                    pool.wait_ge(o_saved, n + 1)
                    nc.gpsimd.tensor_tensor(uOE[:, j, 0, 1:], uOE[:, j, 1, 1:], uV[:, j, :], ALU.mult)\
                        .then_inc(ev_done, 1)
                for j in range(2):
                    n = UNITS * b + 2 * pair + j
                    pool.wait_ge(r_done, n + 1)
                    pool.wait_ge(ev_done, n + 1)
                    nc.gpsimd.tensor_tensor(uV[:, j, :], uR[:, j, :], uV[:, j, :], ALU.mult)\
                        .then_inc(rv_done, 1)
                    pool.wait_ge(rv_done, n + 1)
                    pool.wait_ge(pq_seeded, n + 1)
                    pool.wait_ge(q_scanned, n + 1)
                    nc.gpsimd.tensor_tensor(uR[:, j, :], uR[:, j, :], before[j][1], ALU.add).then_inc(den_done, 1)
                for j in range(2):
                    n = UNITS * b + 2 * pair + j
                    pool.wait_ge(p_scanned, n + 1)
                    nc.gpsimd.tensor_tensor(uV[:, j, :], uV[:, j, :], before[j][0], ALU.add).then_inc(num_done, 1)

            def lo_piece(g):
                pool.wait_ge(ws_done, g + 1)
                nc.gpsimd.tensor_tensor(W[:, (g // Q) % 2, 1, g % Q, :], rings[g // NB][ring_slot(g)[0]],
                                        W[:, (g // Q) % 2, 0, g % Q, :], ALU.subtract).then_inc(lo_done, 1)

            for T in range(HT):
                rstd_of(0, T)
            products(0, 0)
            for g in (0, 1):
                lo_piece(g)
            products(0, 1)
            for g in (2, 3, 4):
                lo_piece(g)
            products(0, 2)
            for g in (5, 6):
                lo_piece(g)
            products(0, 3)
            lo_piece(7)
            for T in range(HT):
                rstd_of(1, T)
            for T in range(HT, TILES):
                rstd_of(0, T)
            for s in range(STEPS):
                for q in range(Q):
                    if 1 <= s < STEPS - 1:
                        lo_piece(Q * (s + 1) + q)
                    if (s, q) in FRONT_P1:
                        products(0, FRONT_P1[s, q])
            for T in range(HT, TILES):
                rstd_of(1, T)
            for T in range(TILES, 2 * TILES):
                rstd_of(0, T)
            for pair in range(HT):
                products(1, pair)
            for q in range(Q):
                lo_piece(NB + q)
            for s in range(STEPS):
                rstd_of(1, TILES + s)
                if s in FRONT_M0:
                    products(1, FRONT_M0[s])
                if s + 1 < STEPS:
                    for q in range(Q):
                        lo_piece(NB + Q * (s + 1) + q)
            with pool.Fori(1, B - 1) as b:
                for s in range(HT):
                    rstd_of(0, TILES * (b + 1) + 2 * s)
                    rstd_of(0, TILES * (b + 1) + 2 * s + 1)
                    if s >= 1:
                        products(b + 1, s - 1)
                with pool.Fori(HT - 1, CB - 1) as pair:
                    products(b + 1, pair)
                rstd_of(1, TILES * (b + 1))
                products(b + 1, CB - 1)
                with pool.Fori(1, TILES) as t:
                    rstd_of(1, TILES * (b + 1) + t)

        @block.scalar
        def _(act):
            act.wait_ge(s_const, 16 * 8)
            nc.scalar.activation(tg[:, :], gates[:, :], ACT.Tanh).then_inc(s_tg, 1)

            def copy_k(b, tile, first=False):
                act.wait_ge(kt_done, TILES * b + tile + 1)
                if not first:
                    act.wait_ge(yt_done, TILES * (b - 1) + (TILES if isinstance(tile, int) and tile >= HT else HT))
                h = tile // HT
                nc.scalar.activation(K[:, CB * h:CB * (h + 1), P * (tile % HT):P * (tile % HT + 1)],
                                     trA[:, :, :], ACT.Copy).then_inc(k_copied, 1)

            def copy_xt(b, tile):
                act.wait_ge(xt_done, TILES * b + tile + 1)
                nc.scalar.activation(XT[:, :, P * tile:P * (tile + 1)], trX[:, :, :], ACT.Copy)\
                    .then_inc(xt_copied, 1)

            def exps(b, pair):
                n = UNITS * b + 2 * pair
                for j in range(2):
                    act.wait_ge(d1_done, n + j + 1)
                    nc.scalar.activation(uOE[:, j, 1, 1:], uOE[:, j, 1, 1:], ACT.Exp).then_inc(e2_done, 1)
                for j in range(2):
                    act.wait_ge(d2_done, n + j + 1)
                    nc.scalar.activation(uA[:, j, :], uA[:, j, :], ACT.Exp).then_inc(a2_done, 1)
                for j in range(2):
                    act.wait_ge(z_done, n + j + 1)
                    nc.scalar.activation(uR[:, j, :], uR[:, j, :], ACT.Exp).then_inc(r_done, 1)

            def hi_piece(g):
                s = g // Q
                v = s if s < STEPS else s + STEPS
                slot, n = ring_slot(g)
                piece = rings[g // NB][slot]
                act.wait_ge(wst_landed[slot], 16 * (n + 1))
                if g % Q == 0 and v >= 2:
                    act.wait_ge(mm_done, groups_through_0(v - 2))
                    act.wait_ge(w_stored[s % 2], 16 * Q * (s // 2))
                nc.scalar.activation(W[:, s % 2, 0, g % Q, :], piece, ACT.Copy, scale=W_SCALE)\
                    .then_inc(hi_done, 1)
                act.wait_ge(hi_done, g + 1)
                nc.scalar.activation(piece, piece, ACT.Copy, scale=W_SCALE)\
                    .then_inc(ws_done, 1)

            def gelu(m, nb, half, bank):
                act.wait_ge(mm_done, m + 1)
                nc.scalar.activation(DT[:, nb, HALF * half:HALF * (half + 1)], acc[bank][:, :], ACT.Gelu,
                                     bias=b0[:, bass.ds(nb, 1)], scale=1.0 / W_SCALE).then_inc(acc_drained, 1)

            def round_e(b, s, half):
                act.wait_ge(mm_done, GROUPS * b + GROUPS1 + 2 * s + half + 1)
                if not (isinstance(b, int) and b == 0 and s == 0):
                    act.wait_ge(et_done, 2 * CB * b + 2 * s + half - 1)
                nc.scalar.activation(e16[:, half, :], acc[(2 * s + half) % BANKS][:, :], ACT.Identity,
                                     bias=b1[:, s:s + 1], scale=1.0 / W_SCALE).then_inc(acc_drained, 1)

            for T in range(HT):
                copy_k(0, T, first=True)
            exps(0, 0)
            for g in (0, 1):
                hi_piece(g)
            exps(0, 1)
            for g in (2, 3, 4):
                hi_piece(g)
            exps(0, 2)
            for g in (5, 6):
                hi_piece(g)
            exps(0, 3)
            hi_piece(7)
            for T in range(HT):
                copy_xt(0, T)
            for s in range(STEPS):
                for q in range(Q):
                    if s == 0:
                        copy_k(0, HT + q, first=True)
                    gelu(Q * s + q, Q * s + q, 0, q)
                    if 1 <= s < STEPS - 1:
                        hi_piece(Q * (s + 1) + q)
                    if (s, q) in FRONT_P1:
                        exps(0, FRONT_P1[s, q])
                    if s >= STEPS - 2:
                        for what, t in POSTS_P1.get((s - STEPS + 2, q), ()):
                            if what == "x2":
                                copy_xt(0, t)
            for s in range(STEPS):
                for q in range(Q):
                    if s == STEPS - 1:
                        hi_piece(NB + q)
                    gelu(NB + Q * s + q, Q * s + q, 1, q)
                    if s < 2:
                        copy_k(1, Q * s + q)
                    if (s, q) in FRONT_P2:
                        exps(1, FRONT_P2[s, q])

            def second_product(b, pairs, split=False, front=True):
                for s in range(STEPS):
                    if s in pairs:
                        exps(b + 1, pairs[s])
                    if split and s + 1 < STEPS:
                        hi_piece(NB + Q * (s + 1))
                        hi_piece(NB + Q * (s + 1) + 1)
                    round_e(b, s, 0)
                    if front:
                        copy_xt(b + 1, s)
                    if split and s + 1 < STEPS:
                        hi_piece(NB + Q * (s + 1) + 2)
                        hi_piece(NB + Q * (s + 1) + 3)
                    round_e(b, s, 1)

            second_product(0, FRONT_M0, split=True)

            def first_product(b, front=True):
                def step(s, tiles, pair):
                    for q in range(Q):
                        for half in range(2):
                            i = 2 * q + half
                            gelu(GROUPS * b + 2 * Q * s + i, Q * s + q, half, i % BANKS)
                            if i in (1, 2) and tiles is not None:
                                copy_k(b + 1, tiles + i - 1)
                            if i == 3 and pair is not None:
                                exps(b + 1, pair)

                for s in range(HT):
                    step(s, 2 * s if front else None, s - 1 if front and s else None)
                with act.Fori(HT, STEPS) as s:
                    step(s, None, s - 1 if front else None)

            with act.Fori(1, B - 1) as b:
                first_product(b)
                second_product(b, {0: CB - 1})
            first_product(B - 1, front=False)
            second_product(B - 1, {}, front=False)

        @block.vector
        def _(dve):
            def norm_stats(i, b, tile, src, normalised):
                T = TILES * b + tile
                first = isinstance(T, int) and T == 0
                if not first:
                    dve.wait_ge(normalised, T)
                    dve.wait_ge(mv_done[i], T)
                both = 2 * T + 2 if isinstance(T, int) else dve.to_reg(2 * T + 2)
                for h in range(2):
                    nc.vector.bn_stats(stats[:, i, h, :], src[:, 512 * h:512 * (h + 1)]).then_inc(bn_done[i], 1)
                dve.wait_ge(s_pool0, 6)
                dve.wait_ge(bn_done[i], both)
                nc.vector.bn_aggr(mv[:, i, :], stats[:, i, :, :].rearrange("p h k -> p (h k)"))\
                    .then_inc(mv_done[i], 1)
                dve.wait_ge(mv_done[i], T + 1)
                nc.vector.tensor_scalar(rstd[:, i, 0:1], mv[:, i, 1:2], EPS, None, ALU.add).then_inc(ve_done[i], 1)

            def normalise(i, b, tile, out, src, sem):
                dve.wait_ge(rstd_done[i], TILES * b + tile + 1)
                nc.vector.tensor_scalar(out, src, mv[:, i, 0:1], rstd[:, i, 1:2], ALU.subtract, ALU.mult)\
                    .then_inc(sem, 1)

            def norm_k(b, tile):
                slot = tile % 2
                if isinstance(b, int) and b == 0 and 2 <= tile < HT:
                    dve.wait_ge(xr_landed[slot], 16)
                else:
                    dve.wait_ge(x_landed[slot], 16 * (HT * b + tile // 2 + (isinstance(b, int) and b == 0 and tile < 2)))
                at = x_tile(TILES * b + tile, slot)
                norm_stats(0, b, tile, at, xn_ready)
                normalise(0, b, tile, at, at, xn_ready)

            def residual(b, tile):
                slot = tile % 2
                dve.wait_ge(yt_done, TILES * b + tile + 1)
                dve.wait_ge(xr_landed[slot], 16 * (HT * b + tile // 2 + 2))
                nc.vector.scalar_tensor_tensor(
                    xres[:, slot, :], trA[:, :, :].rearrange("p c h -> p (c h)"), tg[:, 0:1],
                    xres[:, slot, :], ALU.mult, ALU.add).then_inc(x2_done, 1)
                dve.wait_ge(x2_done, TILES * b + tile + 1)
                norm_stats(1, b, tile, xres[:, slot, :], xh_ready)

            def norm_x2(b, tile):
                if not (isinstance(b, int) and b == 0 and tile == 0):
                    dve.wait_ge(xt_done, TILES * b + tile)
                normalise(1, b, tile, xh[:, :], xres[:, tile % 2, :], xh_ready)

            def units(b, pair):
                n = UNITS * b + 2 * pair
                first = isinstance(n, int) and n == 0
                u = [2 * pair + j for j in range(2)]
                k = [K[:, u[j], :] for j in range(2)]
                before = [[uOE[:, j, i, 0:HALF] for i in range(2)] for j in range(2)]
                now = [[uOE[:, j, i, 1:] for i in range(2)] for j in range(2)]
                for j in range(2):
                    if not first:
                        dve.wait_ge(y_done, n + j - 1)
                        dve.wait_ge(o_saved, n + j - 1)
                    nc.vector.tensor_copy(uOE[:, j, 0, 0:1], st_o[:, bass.ds(u[j], 1)]).then_inc(o_seeded, 1)
                for j in range(2):
                    nc.vector.tensor_tensor_scan(now[j][0], w_u[:, 0, bass.ds(u[j], 1)].to_broadcast([P, HALF]),
                                                 k[j], st_o[:, bass.ds(u[j], 1)], ALU.add, ALU.max)\
                        .then_inc(o_scanned, 1)
                for j in range(2):
                    dve.wait_ge(o_scanned, n + j + 1)
                    nc.vector.tensor_tensor(now[j][1], k[j], now[j][0], ALU.subtract).then_inc(d1_done, 1)
                for j in range(2):
                    dve.wait_ge(o_seeded, n + j + 1)
                    nc.vector.scalar_tensor_tensor(uA[:, j, :], before[j][0], w_u[:, 0, bass.ds(u[j], 1)],
                                                   now[j][0], ALU.add, ALU.subtract).then_inc(d2_done, 1)
                for j in range(2):
                    nc.vector.scalar_tensor_tensor(uR[:, j, :], k[j], w_u[:, 1, bass.ds(u[j], 1)],
                                                   before[j][0], ALU.add, ALU.subtract).then_inc(z_raw, 1)
                for j in range(2):
                    nc.vector.tensor_copy(st_o[:, bass.ds(u[j] + CB, 1)], uOE[:, j, 0, HALF:]).then_inc(o_saved, 1)
                for j in range(2):
                    dve.wait_ge(z_raw, n + j + 1)
                    nc.vector.tensor_scalar(uR[:, j, :], uR[:, j, :], R_CAP, None, ALU.min).then_inc(z_done, 1)
                for j in range(2):
                    dve.wait_ge(d2_done, n + j + 1)
                    if not first:
                        dve.wait_ge(pq_saved, n + j - 1)
                    nc.vector.tensor_copy(uOE[:, j, :, 0], st_pq[:, u[j], :]).then_inc(pq_seeded, 1)
                for j in range(2):
                    dve.wait_ge(a2_done, n + j + 1)
                    dve.wait_ge(ev_done, n + j + 1)
                    nc.vector.tensor_tensor_scan(now[j][1], uA[:, j, :], now[j][1],
                                                 st_pq[:, u[j], 1:2], ALU.mult, ALU.add).then_inc(q_scanned, 1)
                for j in range(2):
                    nc.vector.tensor_tensor_scan(now[j][0], uA[:, j, :], now[j][0],
                                                 st_pq[:, u[j], 0:1], ALU.mult, ALU.add).then_inc(p_scanned, 1)
                for j in range(2):
                    dve.wait_ge(p_scanned, n + j + 1)
                    nc.vector.tensor_copy(st_pq[:, u[j] + CB, :], uOE[:, j, :, HALF]).then_inc(pq_saved, 1)
                for j in range(2):
                    dve.wait_ge(den_done, n + j + 1)
                    nc.vector.reciprocal(uR[:, j, :], uR[:, j, :]).then_inc(rec_done, 1)
                for j in range(2):
                    dve.wait_ge(rec_done, n + j + 1)
                    dve.wait_ge(num_done, n + j + 1)
                    nc.vector.tensor_tensor(k[j], uV[:, j, :], uR[:, j, :], ALU.mult).then_inc(y_done, 1)

            def add_out(b, s, half):
                dve.wait_ge(et_done, 2 * CB * b + 2 * s + half + 1)
                dve.wait_ge(xo_landed[s % 2], 16 * (CB // 2 * b + s // 2 + 1))
                o = xo[:, s % 2, HT * half:HT * (half + 1), :].rearrange("p t h -> p (t h)")
                nc.vector.scalar_tensor_tensor(o, trE[:, :, :].rearrange("p t h -> p (t h)"), tg[:, 1:2], o,
                                               ALU.mult, ALU.add).then_inc(out_added, 1)

            def posts(b, tiles):
                for t in tiles:
                    residual(b, t)
                    norm_x2(b, t)

            for t in range(HT):
                norm_k(0, t)
            dve.wait_ge(s_const, 16 * 8)
            dve.wait_ge(s_pool0, 6)
            dve.wait_ge(k_copied, HT)
            for pair in range(HT):
                units(0, pair)
            dve.wait_ge(s_tg, 1)
            posts(0, range(HT))
            for t in range(HT, TILES):
                norm_k(0, t)
            dve.wait_ge(k_copied, TILES)
            for pair in range(HT, 2 * HT):
                units(0, pair)
            posts(0, range(HT, TILES))
            for t in range(TILES):
                norm_k(1, t)
            dve.wait_ge(k_copied, 2 * TILES)
            for pair in range(HT):
                units(1, pair)

            def second_product(b, pairs, front=True):
                for s in range(STEPS):
                    if front:
                        residual(b + 1, s)
                    if s >= 1:
                        add_out(b, s - 1, 1)
                    if front:
                        norm_x2(b + 1, s)
                    if s in pairs:
                        units(b + 1, pairs[s])
                    add_out(b, s, 0)

            second_product(0, FRONT_M0)

            def first_product(b, front=True):
                if not front:
                    add_out(b - 1, STEPS - 1, 1)
                    return
                for s in range(HT):
                    norm_k(b + 1, 2 * s)
                    if s == 0:
                        add_out(b - 1, STEPS - 1, 1)
                    norm_k(b + 1, 2 * s + 1)
                    if s >= 1:
                        if s == 1:
                            dve.wait_ge(k_copied, TILES * (b + 1) + HT)
                        units(b + 1, s - 1)
                with dve.Fori(HT - 1, CB - 1) as pair:
                    dve.wait_ge(k_copied, TILES * (b + 2))
                    units(b + 1, pair)

            with dve.Fori(1, B - 1) as b:
                first_product(b)
                second_product(b, {0: CB - 1})
            first_product(B - 1, front=False)
            second_product(B - 1, {}, front=False)
            add_out(B - 1, STEPS - 1, 1)

        @block.tensor
        def _(pe):
            def transpose_k(b, tile, slot):
                T = TILES * b + tile
                pe.wait_ge(xn_ready, T + 1)
                if not (isinstance(T, int) and T == 0):
                    pe.wait_ge(k_copied, T)
                    if not (isinstance(b, int) and b == 0 and tile < HT):
                        pe.wait_ge(x2_done, HT if isinstance(b, int) and b == 0 else TILES * b)
                for c in range(CB):
                    mm = nc.tensor.transpose(trA[:, c, :], x_tile(T, slot)[:, P * c:P * (c + 1)], ident[:, :])
                mm.then_inc(kt_done, 1)

            def transpose_y(b, tile):
                T = TILES * b + tile
                h = tile // HT
                pe.wait_ge(y_done, UNITS * b + CB * (h + 1))
                pe.wait_ge(k_copied, HT if isinstance(T, int) and T < HT else TILES * (b + 1))
                if not (isinstance(T, int) and T == 0):
                    pe.wait_ge(x2_done, T)
                for c in range(CB):
                    mm = nc.tensor.transpose(trA[:, c, :], K[:, CB * h + c, P * (tile % HT):P * (tile % HT + 1)],
                                             ident[:, :])
                mm.then_inc(yt_done, 1)

            def transpose_x2(b, tile):
                T = TILES * b + tile
                pe.wait_ge(xh_ready, T + 1)
                if not (isinstance(T, int) and T == 0):
                    pe.wait_ge(xt_copied, T)
                for c in range(CB):
                    mm = nc.tensor.transpose(trX[:, c, :], xh[:, P * c:P * (c + 1)], ident16[:, :])
                mm.then_inc(xt_done, 1)

            def transpose_e(b, s, half):
                n = 2 * CB * b + 2 * s + half
                pe.wait_ge(acc_drained, GROUPS * b + GROUPS1 + 2 * s + half + 1)
                if not (isinstance(n, int) and n == 0):
                    pe.wait_ge(out_added, n)
                for t in range(HT):
                    mm = nc.tensor.transpose(trE[:, t, :], e16[:, half, P * t:P * (t + 1)], ident16[:, :])
                mm.then_inc(et_done, 1)

            def group1(m, slot, q, half, bank):
                if not (isinstance(m, int) and m < BANKS):
                    pe.wait_ge(acc_drained, m - BANKS + 1)
                for c in range(CB):
                    for part in range(2):
                        mm = nc.tensor.matmul(acc[bank][:, :], W[:, slot, part, q, P * c:P * (c + 1)],
                                              XT[:, c, HALF * half:HALF * (half + 1)],
                                              start=(c == 0 and part == 0), stop=(c == CB - 1 and part == 1))
                mm.then_inc(mm_done, 1)

            def second_product(b, front=True):
                for s in range(STEPS):
                    slot = s % 2
                    split = isinstance(b, int) and b == 0
                    if not split:
                        pe.wait_ge(w_landed[slot], 16 * (Q + CB * (b - 1) + Q + s // 2 + 1))
                    for half in range(2):
                        m = GROUPS * b + GROUPS1 + 2 * s + half
                        bank = (2 * s + half) % BANKS
                        if front and half == 0:
                            transpose_y(b + 1, s)
                        pe.wait_ge(acc_drained, m - BANKS + 1)
                        if front and half == 1:
                            transpose_x2(b + 1, s)
                        for q in range(Q):
                            if split and half == 0:
                                pe.wait_ge(lo_done, NB + Q * s + q + 1)
                            if s == 0 and half == 0 and q == Q - 1:
                                pe.wait_ge(acc_drained, GROUPS * b + GROUPS1)
                            for c in range(CB):
                                nb = CB * q + c
                                for part in range(2):
                                    mm = nc.tensor.matmul(
                                        acc[bank][:, :], W[:, slot, part, q, P * c:P * (c + 1)],
                                        DT[:, nb, HALF * half:HALF * (half + 1)],
                                        start=(nb == 0 and part == 0), stop=(nb == NB - 1 and part == 1))
                            if q == 0 and (s, half) != (0, 0):
                                transpose_e(b, *((s, 0) if half else (s - 1, 1)))
                        mm.then_inc(mm_done, 1)

            pe.wait_ge(s_pool0, 6)
            for t in range(HT):
                transpose_k(0, t, t % 2)
            posts = [("y", 0), ("y", 1), ("x", 0), ("y", 2), ("x", 1), ("y", 3), ("x", 2), ("x", 3)]
            for what, t in posts:
                (transpose_y if what == "y" else transpose_x2)(0, t)
            pe.wait_ge(xt_copied, HT)
            for s in range(2):
                for q in range(Q):
                    pe.wait_ge(lo_done, Q * s + q + 1)
                    group1(Q * s + q, s, q, 0, q)
                    if s == 0:
                        transpose_k(0, HT + q, q % 2)

            def split_steps(p, posts_at):
                for slot in range(2):
                    for q in range(Q):
                        m = 2 * Q * p + Q * slot + q
                        pe.wait_ge(lo_done, m + 1)
                        group1(m, slot, q, 0, q)
                        for what, t in posts_at.get((slot, q), ()):
                            (transpose_y if what == "y" else transpose_x2)(0, t)

            with pe.Fori(1, STEPS // 2 - 1) as p:
                split_steps(p, {})
            split_steps(STEPS // 2 - 1, POSTS_P1)
            pe.wait_ge(xt_copied, TILES)
            for s in range(2):
                pe.wait_ge(w_landed[s], 16)
                for q in range(Q):
                    group1(NB + Q * s + q, s, q, 1, q)
                    transpose_k(1, Q * s + q, q % 2)
            with pe.Fori(1, STEPS // 2) as p:
                for slot in range(2):
                    pe.wait_ge(w_landed[slot], 16 * p + 16)
                    for q in range(Q):
                        group1(NB + 2 * Q * p + Q * slot + q, slot, q, 1, q)
            second_product(0)

            def first_product(b, front=True):
                pe.wait_ge(xt_copied, TILES * (b + 1))

                def pair_of_steps(p, tiles, pending=False):
                    for slot in range(2):
                        pe.wait_ge(w_landed[slot], 16 * (Q + CB * (b - 1) + p + 1))
                        for i in range(2 * Q):
                            m = GROUPS * b + 4 * Q * p + 2 * Q * slot + i
                            group1(m, slot, i // 2, i % 2, i % BANKS)
                            if pending and slot == 0 and i == 0:
                                transpose_e(b - 1, STEPS - 1, 1)
                            if tiles and i in (1, 2):
                                transpose_k(b + 1, 4 * p + 2 * slot + i - 1, i - 1)

                pair_of_steps(0, front, pending=True)
                pair_of_steps(1, front)
                with pe.Fori(2, STEPS // 2) as p:
                    pair_of_steps(p, False)

            with pe.Fori(1, B - 1) as b:
                first_product(b)
                second_product(b)
            first_product(B - 1, front=False)
            second_product(B - 1, front=False)
            transpose_e(B - 1, STEPS - 1, 1)


V_P1 = {12: 5, 18: 6, 23: 7}
FRONT_P1 = {(1, 1): 4, (2, 2): 5, (3, 3): 6, (5, 0): 7}
FRONT_P2 = {(2, 1): 0, (3, 2): 1, (4, 3): 2, (6, 0): 3}
FRONT_M0 = {0: 4, 1: 5, 2: 6, 3: 7}
POSTS_P1 = {(1, 0): [("y", 4)], (1, 1): [("y", 5), ("x2", 4)], (1, 2): [("y", 6), ("x2", 5)],
            (1, 3): [("y", 7), ("x2", 6), ("x2", 7)]}


def kernel(x, ctx_2048, g_xattn, g_ffn, L0_xattn_w, L0_xattn_u, L0_ffn_W0, L0_ffn_bias0, L0_ffn_W1,
           L0_ffn_bias1):
    import concourse.bacc as bacc
    from concourse.bass_utils import run_bass_kernel_spmd

    def blocks(v, n):
        return np.asarray(v).reshape(n, P).T

    arrays = {
        "x": np.asarray(x).reshape(B * TILES, P, H),
        "vT": np.asarray(ctx_2048).reshape(B, 2, HALF, CB, P).transpose(0, 1, 3, 4, 2).reshape(B, UNITS, P, HALF),
        "g_xattn": np.broadcast_to(np.asarray(g_xattn).reshape(1, 1), (P, 1)),
        "g_ffn": np.broadcast_to(np.asarray(g_ffn).reshape(1, 1), (P, 1)),
        "w": blocks(L0_xattn_w, CB),
        "u": blocks(L0_xattn_u, CB),
        "w0": np.asarray(L0_ffn_W0).reshape(NB, P, CB, P).transpose(0, 3, 2, 1).reshape(NB, P, 1024),
        "bias0": blocks(L0_ffn_bias0, NB),
        "w1": np.asarray(L0_ffn_W1).reshape(CB, P, Q, CB, P).transpose(0, 2, 4, 3, 1).reshape(NB, P, 1024),
        "bias1": blocks(L0_ffn_bias1, CB),
    }
    arrays = {n: np.ascontiguousarray(a) for n, a in arrays.items()}
    nc = bacc.Bacc("TRN2", target_bir_lowering=False, num_devices=1)
    args = {n: nc.dram_tensor(f"{n}_in", a.shape, mybir.dt.from_np(a.dtype), kind="ExternalInput").ap()
            for n, a in arrays.items()}
    out = nc.dram_tensor("out", (B, CB, P, TILES, P), F32, kind="ExternalOutput").ap()
    build(nc, **args, out=out)
    r = run_bass_kernel_spmd(nc, [{f"{n}_in": a for n, a in arrays.items()}], core_ids=[0])
    return r.results[0]["out"].transpose(0, 3, 2, 1, 4).reshape(B, L, H)
```

```python
from contextlib import ExitStack

import numpy as np
import concourse.bass as bass
from concourse import mybir

ALU = mybir.AluOpType
ACT = mybir.ActivationFunctionType
F32 = mybir.dt.float32
F16 = mybir.dt.float16

P = 128
B, L, H, N = 4, 1024, 1024, 4096
CB = H // P
TILES = L // P
HALF = 512
HT = HALF // P
UNITS = 2 * CB
NB = N // P
Q = 4
STEPS = NB // Q
assert STEPS == CB == 8 and TILES == 8
GROUPS1 = 2 * NB
GROUPS = GROUPS1 + 2 * CB
BANKS = 4
EPS = 1e-5
NEG_INF = -1e38
R_CAP = 60.0
W_SCALE = 1024.0


def groups_through(b, step):
    if step < STEPS:
        return GROUPS * b + 2 * Q * (step + 1)
    return GROUPS * b + GROUPS1 + 2 * (step - STEPS + 1)


def groups_through_0(v):
    if v < 2 * STEPS:
        return Q * (v + 1)
    return GROUPS1 + 2 * (v - 2 * STEPS + 1)


def build(nc, x, xT, vT, g_xattn, g_ffn, w, u, w0, bias0, w1, bias1, out):
    x2_dram = nc.dram_tensor("x2_dram", (B, CB, P, 2, HALF), F32).ap()
    x2_view = x2_dram.rearrange("b (h c) p u t -> b c u p h t", h=2)
    parts_dram = nc.dram_tensor("parts_dram", (2 * STEPS, P, 2 * Q * 1024), F16).ap()

    with ExitStack() as ctx:
        def sb(name, shape, dt=F32):
            return ctx.enter_context(nc.sbuf_tensor(name, shape, dt))

        def ps(name, shape, dt=F32):
            return ctx.enter_context(nc.psum_tensor(name, shape, dt))

        def sem(name):
            return ctx.enter_context(nc.semaphore(name))

        def sems(name, n=2):
            return [sem(f"{name}{i}") for i in range(n)]

        ident = sb("ident", [P, P])
        ident16 = sb("ident16", [P, P], F16)
        gates = sb("gates", [P, 2])
        tg = sb("tg", [P, 2])
        power = sb("power", [P, 1])
        w_u = sb("w_u", [P, 2, UNITS])
        b0 = sb("b0", [P, NB])
        b1 = sb("b1", [P, CB])
        xin = sb("xin", [P, 2, H])
        xT2 = sb("xT2", [P, 2, 2, HALF])
        xh = sb("xh", [P, H], F16)
        stats = sb("stats", [P, 2, 2, 6])
        mv = sb("mv", [P, 2, 2, 2])
        rstd = sb("rstd", [P, 2, 2, 2])
        K = sb("K", [P, UNITS, HALF])
        uV = sb("uV", [P, 2, HALF])
        uOE = sb("uOE", [P, 2, 2, HALF + 1])
        uA = sb("uA", [P, 2, HALF])
        uR = sb("uR", [P, 2, HALF])
        st_o = sb("st_o", [P, UNITS + CB])
        st_pq = sb("st_pq", [P, UNITS + CB, 2])
        XT = sb("XT", [P, CB, L], F16)
        DT = sb("DT", [P, NB, L], F16)
        stage = sb("stage", [P, 3, 1024])
        W = sb("W", [P, 2, 2, Q, 1024], F16)
        e16 = sb("e16", [P, 2, HALF], F16)
        xo = sb("xo", [P, 2, L])

        rings = [[stage[:, i, :] for i in range(3)] + [xo[:, i, :] for i in range(2)],
                 [stage[:, i, :] for i in range(3)]]

        def ring_slot(g):
            before = [k % 5 if k < NB else k % 3 for k in range(g)]
            slot = g % 5 if g < NB else g % 3
            return slot, before.count(slot)

        def x_tile(T, slot):
            if isinstance(T, int) and 2 <= T < HT:
                return xT2[:, slot, :, :].rearrange("p u t -> p (u t)")
            return xin[:, slot, :]

        acc = [ps(f"acc{i}", [P, HALF]) for i in range(BANKS)]
        trA = ps("trA", [P, CB, P])
        trX = ps("trX", [P, CB, P], F16)

        def in_acc(b, tile):
            return isinstance(b, int) and b == 0 and tile in (1, 3)

        def tokens_at(b, tile):
            if in_acc(b, tile):
                return [acc[2][:, :], acc[3][:, :]]
            return [trA[:, c:c + CB // 2, :].rearrange("p c h -> p (c h)") for c in (0, CB // 2)]

        s_const = sem("const_landed")
        s_tg = sem("tg_ready")
        s_pool0 = sem("pool_constants")
        x_landed, xT_landed, v_landed = sems("x_landed"), sems("xT_landed"), sems("v_landed")
        x2_stored, xo_landed, out_stored = sem("x2_stored"), sems("xo_landed"), sems("out_stored")
        wst_landed, w_landed, w_stored = sems("wst_landed", 5), sems("w_landed"), sems("w_stored")
        bn_done, mv_done, ve_done, rstd_done = (sems(n) for n in ("bn_done", "mv_done", "ve_done", "rstd_done"))
        xn_ready, kt_done, k_copied = sem("xn_ready"), sem("kt_done"), sem("k_copied")
        x2t_done, x2_done, xh_ready = sem("x2t_done"), sem("x2_done"), sem("xh_ready")
        xt_done, xt_copied = sem("xt_done"), sem("xt_copied")
        o_seeded, o_scanned, o_saved = sem("o_seeded"), sem("o_scanned"), sem("o_saved")
        d1_done, d2_done, z_raw, z_done = sem("d1_done"), sem("d2_done"), sem("z_raw"), sem("z_done")
        e2_done, a2_done, r_done = sem("e2_done"), sem("a2_done"), sem("r_done")
        ev_done, rv_done = sem("ev_done"), sem("rv_done")
        pq_seeded, q_scanned, p_scanned, pq_saved = (sem(n) for n in ("pq_seeded", "q_scanned", "p_scanned", "pq_saved"))
        den_done, num_done, rec_done, y_done = sem("den_done"), sem("num_done"), sem("rec_done"), sem("y_done")
        hi_done, ws_done, lo_done = sem("hi_done"), sem("ws_done"), sem("lo_done")
        mm_done, acc_drained = sem("mm_done"), sem("acc_drained")
        out_added = sem("out_added")

        block = ctx.enter_context(nc.Block())

        @block.sync
        def _(sp):
            def load_x(T, slot):
                if isinstance(T, int) and 2 <= T < HT:
                    sp.dma_start(x_tile(T, slot), x[T]).then_inc(xT_landed[slot], 16)
                    return
                if not (isinstance(T, int) and T < 2):
                    sp.wait_ge(kt_done, T - HT + 1 if isinstance(T, int) and T < HT + 2 else T - 1)
                sp.dma_start(x_tile(T, slot), x[T]).then_inc(x_landed[slot], 16)

            def load_v(b, pair):
                for j in range(2):
                    if not (isinstance(b, int) and isinstance(pair, int) and b == 0 and pair == 0):
                        sp.wait_ge(y_done, UNITS * b + 2 * pair + j - 1)
                    sp.dma_start(uV[:, j, :], vT[b, 2 * pair + j]).then_inc(v_landed[j], 16)

            def load_xT(b, pair, slot):
                if isinstance(b, int) and isinstance(pair, int) and b == 0 and pair < 2:
                    sp.wait_ge(kt_done, pair + 3)
                else:
                    sp.wait_ge(x2_done, CB * b + pair - 1)
                sp.dma_start(xT2[:, slot, :, :], xT[b, pair]).then_inc(xT_landed[slot], 16)

            def store_x2(b, pair):
                sp.wait_ge(x2_done, CB * b + pair + 1)
                sp.dma_start(x2_dram[b, pair], K[:, bass.ds(2 * pair, 2), :]).then_inc(x2_stored, 16)

            def load_pair(b, pair, slot=None):
                load_v(b, pair)
                if not (isinstance(pair, int) and pair == 0):
                    store_x2(b, pair - 1)
                load_xT(b, pair, pair % 2 if slot is None else slot)

            def load_piece(g):
                slot, n = ring_slot(g)
                if n:
                    last = g - 5 if g < NB else g - 3
                    sp.wait_ge(lo_done, NB if last < NB <= g else last + 1)
                src = w0[g] if g < NB else w1[g - NB]
                sp.dma_start(rings[g // NB][slot], src).then_inc(wst_landed[slot], 16)

            def store_piece(g):
                s = g // Q
                sp.wait_ge(lo_done, g + 1)
                sp.dma_start(parts_dram[s].rearrange("p (a q n) -> p a q n", a=2, q=Q)[:, :, g % Q, :],
                             W[:, s % 2, :, g % Q, :]).then_inc(w_stored[s % 2], 16)

            def turn_piece(g):
                ahead = 5 if g < NB else 3
                if g + ahead < (NB if g < NB else 2 * NB):
                    load_piece(g + ahead)
                store_piece(g)

            def load_parts(s, slot, groups):
                sp.wait_ge(mm_done, groups)
                sp.dma_start(W[:, slot, :, :, :].rearrange("p a q n -> p (a q n)"), parts_dram[s])\
                    .then_inc(w_landed[slot], 16)

            for T in range(HT):
                load_x(T, T % 2)
            load_v(0, 0)
            sp.dma_start(w_u[:, 0, 0:CB], w).then_inc(s_const, 16)
            sp.dma_start(w_u[:, 0, CB:UNITS], w).then_inc(s_const, 16)
            sp.dma_start(w_u[:, 1, 0:CB], u).then_inc(s_const, 16)
            sp.dma_start(w_u[:, 1, CB:UNITS], u).then_inc(s_const, 16)
            sp.dma_start(gates[:, 0:1], g_xattn).then_inc(s_const, 16)
            sp.dma_start(gates[:, 1:2], g_ffn).then_inc(s_const, 16)
            sp.dma_start(b0[:, :], bias0).then_inc(s_const, 16)
            sp.dma_start(b1[:, :], bias1).then_inc(s_const, 16)
            load_x(4, 0)
            load_x(5, 1)
            load_xT(0, 0, 0)
            for g in range(5):
                load_piece(g)
            for item in ("v1", 0, 1, "v2", 2, 3, 4, "v3", 5, 6, 7):
                if isinstance(item, int):
                    turn_piece(item)
                else:
                    load_pair(0, int(item[1]))
            load_pair(0, 4)
            load_x(6, 0)
            load_x(7, 1)
            for g in range(2 * Q, NB):
                if g in V_P1:
                    load_pair(0, V_P1[g])
                turn_piece(g)
            load_x(8, 0)
            load_x(9, 1)
            store_x2(0, CB - 1)
            for slot in range(2):
                sp.wait_ge(w_stored[slot], 16 * NB // 2)
            load_parts(0, 0, groups_through_0(STEPS - 2))
            load_x(TILES + 2, 0)
            load_parts(1, 1, groups_through_0(STEPS - 1))
            for T in range(TILES + 3, TILES + 7):
                load_x(T, T % 2)
            load_parts(2, 0, groups_through_0(STEPS))
            load_x(2 * TILES - 1, 1)
            load_pair(1, 0)
            sp.wait_ge(x2_stored, 16 * CB)
            for s in range(3, STEPS):
                load_parts(s, s % 2, groups_through_0(STEPS + s - 2))
                if s == 3:
                    for g in range(NB, NB + 3):
                        load_piece(g)
                else:
                    load_pair(1, s - 3)
            for g in range(NB, NB + Q):
                turn_piece(g)

            def store_out(b, s):
                sp.wait_ge(out_added, 2 * CB * b + 2 * (s + 1))
                sp.dma_start(out[b, s], xo[:, s % 2, :]).then_inc(out_stored[s % 2], 16)

            def second_product(b, pairs, split=False, front=True, more=True):
                for s in range(STEPS):
                    if s in pairs:
                        load_pair(b + 1, pairs[s])
                    if not split and s + 1 < STEPS:
                        load_parts(STEPS + s + 1, (s + 1) % 2, groups_through(b, STEPS + s - 1))
                    if s + 1 == STEPS and more:
                        if split:
                            for slot in range(2):
                                sp.wait_ge(w_stored[slot], 16 * NB)
                        load_parts(0, 0, groups_through(b, 2 * STEPS - 2))
                    if not (isinstance(b, int) and b == 0 and s < 2):
                        sp.wait_ge(out_stored[s % 2], 64 * b + 16 * (s // 2))
                    sp.dma_start(xo[:, s % 2, :].rearrange("p (h t) -> p h t", h=2), x2_view[b, s // 2, s % 2])\
                        .then_inc(xo_landed[s % 2], 16)
                    if front and s - 2 == max(pairs):
                        store_x2(b + 1, CB - 1)
                    if split and s + 1 < STEPS:
                        for g in range(NB + Q * (s + 1), NB + Q * (s + 2)):
                            turn_piece(g)
                    if s >= 1:
                        store_out(b, s - 1)

            second_product(0, {s: FRONT_M0[s] for s in range(1, HT)}, split=True)

            def first_product(b, front=True):
                nb = b + 1
                sp.wait_ge(x2_stored, 16 * CB * (b + 1))

                def step(s, j):
                    load_parts(s + 1, (j + 1) % 2, GROUPS * b + 2 * Q * s)

                for s in range(HT):
                    if front:
                        load_x(TILES * nb + 2 * s, 0)
                        load_x(TILES * nb + 2 * s + 1, 1)
                    step(s, s % 2)
                    if front and s >= 1:
                        load_pair(nb, s - 1)
                    if s == 0:
                        store_out(b - 1, STEPS - 1)
                with sp.Fori(HT // 2, STEPS // 2) as p:
                    for j in range(2):
                        step(2 * p + j, j)
                        if front:
                            load_pair(nb, 2 * p + j - 1, 1 - j)

            with sp.Fori(1, B - 1) as b:
                first_product(b)
                second_product(b, {0: 7})
            first_product(B - 1, front=False)
            second_product(B - 1, {}, front=False, more=False)
            store_out(B - 1, STEPS - 1)
            for slot in range(2):
                sp.wait_ge(out_stored[slot], 64 * B)

        @block.gpsimd
        def _(pool):
            nc.gpsimd.memset(ident[:, :], 0.0).then_inc(s_pool0, 1)
            nc.gpsimd.memset(power[:, :], -0.5).then_inc(s_pool0, 1)
            nc.gpsimd.memset(st_o[:, :], NEG_INF).then_inc(s_pool0, 1)
            nc.gpsimd.memset(st_pq[:, :, :], 0.0).then_inc(s_pool0, 1)
            pool.wait_ge(s_pool0, 4)
            nc.gpsimd.affine_select(out=ident[:, :], in_=ident[:, :], compare_op=ALU.not_equal, fill=1.0,
                                    base=0, pattern=[[-1, P]], channel_multiplier=1).then_inc(s_pool0, 1)
            pool.wait_ge(s_pool0, 5)
            nc.gpsimd.tensor_copy(ident16[:, :], ident[:, :]).then_inc(s_pool0, 1)

            def rstd_of(i, T, odd=None):
                odd = T % 2 if odd is None else odd
                pool.wait_ge(ve_done[i], T + 1)
                nc.gpsimd.tensor_tensor(rstd[:, i, odd, 1:2], rstd[:, i, odd, 0:1], power[:, :], ALU.pow)\
                    .then_inc(rstd_done[i], 1)

            def products(b, pair):
                before = [[uOE[:, j, i, 0:HALF] for i in range(2)] for j in range(2)]
                for j in range(2):
                    n = UNITS * b + 2 * pair + j
                    pool.wait_ge(e2_done, n + 1)
                    pool.wait_ge(v_landed[j], 16 * (CB * b + pair + 1))
                    pool.wait_ge(d2_done, n + 1)
                    pool.wait_ge(z_raw, n + 1)
                    pool.wait_ge(o_saved, n + 1)
                    nc.gpsimd.tensor_tensor(uOE[:, j, 0, 1:], uOE[:, j, 1, 1:], uV[:, j, :], ALU.mult)\
                        .then_inc(ev_done, 1)
                for j in range(2):
                    n = UNITS * b + 2 * pair + j
                    pool.wait_ge(r_done, n + 1)
                    pool.wait_ge(ev_done, n + 1)
                    nc.gpsimd.tensor_tensor(uV[:, j, :], uR[:, j, :], uV[:, j, :], ALU.mult)\
                        .then_inc(rv_done, 1)
                    pool.wait_ge(rv_done, n + 1)
                    pool.wait_ge(pq_seeded, n + 1)
                    pool.wait_ge(q_scanned, n + 1)
                    nc.gpsimd.tensor_tensor(uR[:, j, :], uR[:, j, :], before[j][1], ALU.add).then_inc(den_done, 1)
                for j in range(2):
                    n = UNITS * b + 2 * pair + j
                    pool.wait_ge(p_scanned, n + 1)
                    nc.gpsimd.tensor_tensor(uV[:, j, :], uV[:, j, :], before[j][0], ALU.add).then_inc(num_done, 1)

            def lo_piece(g):
                pool.wait_ge(ws_done, g + 1)
                nc.gpsimd.tensor_tensor(W[:, (g // Q) % 2, 1, g % Q, :], rings[g // NB][ring_slot(g)[0]],
                                        W[:, (g // Q) % 2, 0, g % Q, :], ALU.subtract).then_inc(lo_done, 1)

            for T in range(HT):
                rstd_of(0, T)
            products(0, 0)
            for g in (0, 1):
                lo_piece(g)
            products(0, 1)
            for g in (2, 3, 4):
                lo_piece(g)
            products(0, 2)
            for g in (5, 6):
                lo_piece(g)
            products(0, 3)
            lo_piece(7)
            for t in (0, 2):
                rstd_of(1, t)
                rstd_of(0, HT + t // 2)
                rstd_of(1, t + 1)
            for T in range(HT + 2, TILES):
                rstd_of(0, T)
            for s in range(STEPS):
                for q in range(Q):
                    if 2 * Q <= Q * s + q + LEAD < NB:
                        lo_piece(Q * s + q + LEAD)
                    if (s, q) in FRONT_P1:
                        products(0, FRONT_P1[s, q])
            for T in range(HT, TILES):
                rstd_of(1, T)
            for T in range(TILES, 2 * TILES):
                rstd_of(0, T)
            for pair in range(HT):
                products(1, pair)
            for q in range(Q):
                lo_piece(NB + q)
            for s in range(STEPS):
                rstd_of(1, TILES + s)
                if s in FRONT_M0:
                    products(1, FRONT_M0[s])
                if s + 1 < STEPS:
                    for q in range(Q):
                        lo_piece(NB + Q * (s + 1) + q)
            with pool.Fori(1, B - 1) as b:
                for s in range(HT):
                    rstd_of(0, TILES * (b + 1) + 2 * s, 0)
                    rstd_of(0, TILES * (b + 1) + 2 * s + 1, 1)
                    if s >= 1:
                        products(b + 1, s - 1)
                with pool.Fori(HT - 1, CB - 1) as pair:
                    products(b + 1, pair)
                rstd_of(1, TILES * (b + 1), 0)
                products(b + 1, CB - 1)
                for t in range(1, TILES):
                    rstd_of(1, TILES * (b + 1) + t, t % 2)

        @block.scalar
        def _(act):
            act.wait_ge(s_const, 16 * 8)
            nc.scalar.activation(tg[:, :], gates[:, :], ACT.Tanh).then_inc(s_tg, 1)

            def copy_k(b, tile, first=False):
                act.wait_ge(kt_done, TILES * b + tile + 1)
                if not first:
                    act.wait_ge(x2_stored, 16 * CB * b)
                h = tile // HT
                columns = slice(P * (tile % HT), P * (tile % HT + 1))
                if in_acc(b, tile):
                    for i in range(2):
                        copied = nc.scalar.activation(K[:, HT * i:HT * (i + 1), columns],
                                                      acc[2 + i][:, :].rearrange("p (c h) -> p c h", c=HT), ACT.Copy)
                    copied.then_inc(k_copied, 1)
                else:
                    nc.scalar.activation(K[:, CB * h:CB * (h + 1), columns], trA[:, :, :], ACT.Copy)\
                        .then_inc(k_copied, 1)

            def copy_xt(b, tile):
                act.wait_ge(xt_done, TILES * b + tile + 1)
                nc.scalar.activation(XT[:, :, P * tile:P * (tile + 1)], trX[:, :, :], ACT.Copy)\
                    .then_inc(xt_copied, 1)

            def exps(b, pair):
                n = UNITS * b + 2 * pair
                for j in range(2):
                    act.wait_ge(d1_done, n + j + 1)
                    nc.scalar.activation(uOE[:, j, 1, 1:], uOE[:, j, 1, 1:], ACT.Exp).then_inc(e2_done, 1)
                    act.wait_ge(d2_done, n + j + 1)
                    nc.scalar.activation(uA[:, j, :], uA[:, j, :], ACT.Exp).then_inc(a2_done, 1)
                for j in range(2):
                    act.wait_ge(z_done, n + j + 1)
                    nc.scalar.activation(uR[:, j, :], uR[:, j, :], ACT.Exp).then_inc(r_done, 1)

            def hi_piece(g):
                s = g // Q
                v = s if s < STEPS else s + STEPS
                slot, n = ring_slot(g)
                piece = rings[g // NB][slot]
                act.wait_ge(wst_landed[slot], 16 * (n + 1))
                if v >= STEPS:
                    if g % Q == 0:
                        act.wait_ge(mm_done, groups_through_0(v - 2))
                elif s >= 2:
                    act.wait_ge(mm_done, g - 2 * Q + 1)
                if g % Q == 0 and s >= 2:
                    act.wait_ge(w_stored[s % 2], 16 * Q * (s // 2))
                nc.scalar.activation(W[:, s % 2, 0, g % Q, :], piece, ACT.Copy, scale=W_SCALE)\
                    .then_inc(hi_done, 1)
                act.wait_ge(hi_done, g + 1)
                nc.scalar.activation(piece, piece, ACT.Copy, scale=W_SCALE)\
                    .then_inc(ws_done, 1)

            def gelu(m, nb, half, bank):
                act.wait_ge(mm_done, m + 1)
                nc.scalar.activation(DT[:, nb, HALF * half:HALF * (half + 1)], acc[bank][:, :], ACT.Gelu,
                                     bias=b0[:, bass.ds(nb, 1)], scale=1.0 / W_SCALE).then_inc(acc_drained, 1)

            def round_e(b, s, half):
                act.wait_ge(mm_done, GROUPS * b + GROUPS1 + 2 * s + half + 1)
                if not (isinstance(b, int) and b == 0 and s == 0):
                    act.wait_ge(out_added, 2 * CB * b + 2 * s + half - 1)
                nc.scalar.activation(e16[:, half, :], acc[(2 * s + half) % BANKS][:, :], ACT.Identity,
                                     bias=b1[:, s:s + 1], scale=1.0 / W_SCALE).then_inc(acc_drained, 1)

            for T in range(HT):
                copy_k(0, T, first=True)
            exps(0, 0)
            for g in (0, 1):
                hi_piece(g)
            exps(0, 1)
            for g in (2, 3, 4):
                hi_piece(g)
            exps(0, 2)
            for g in (5, 6):
                hi_piece(g)
            exps(0, 3)
            hi_piece(7)
            for T in range(HT):
                copy_xt(0, T)
            copy_k(0, HT, first=True)
            for s in range(STEPS):
                for q in range(Q):
                    if s == 0 and q >= 1:
                        copy_k(0, HT + q, first=True)
                    if 2 * Q <= Q * s + q + LEAD < NB:
                        hi_piece(Q * s + q + LEAD)
                    gelu(Q * s + q, Q * s + q, 0, q)
                    if (s, q) in FRONT_P1:
                        exps(0, FRONT_P1[s, q])
                    if s >= STEPS - 2:
                        for what, t in POSTS_P1.get((s - STEPS + 2, q), ()):
                            if what == "x2":
                                copy_xt(0, t)
            copy_k(1, 0)
            for s in range(STEPS):
                for q in range(Q):
                    if s == STEPS - 1:
                        hi_piece(NB + q)
                    gelu(NB + Q * s + q, Q * s + q, 1, q)
                    if Q * s + q + 1 < TILES:
                        copy_k(1, Q * s + q + 1)
                    if (s, q) in FRONT_P2:
                        exps(1, FRONT_P2[s, q])

            def second_product(b, pairs, split=False, front=True):
                for s in range(STEPS):
                    if s in pairs:
                        exps(b + 1, pairs[s])
                    if split and s + 1 < STEPS:
                        hi_piece(NB + Q * (s + 1))
                        hi_piece(NB + Q * (s + 1) + 1)
                    round_e(b, s, 0)
                    if front:
                        copy_xt(b + 1, s)
                    if split and s + 1 < STEPS:
                        hi_piece(NB + Q * (s + 1) + 2)
                        hi_piece(NB + Q * (s + 1) + 3)
                    round_e(b, s, 1)

            second_product(0, FRONT_M0, split=True)

            def first_product(b, front=True):
                def step(s, tiles, pair):
                    for q in range(Q):
                        for half in range(2):
                            i = 2 * q + half
                            gelu(GROUPS * b + 2 * Q * s + i, Q * s + q, half, i % BANKS)
                            if i in (1, 2) and tiles is not None:
                                copy_k(b + 1, tiles + i - 1)
                            if i == 3 and pair is not None:
                                exps(b + 1, pair)

                for s in range(HT):
                    step(s, 2 * s if front else None, s - 1 if front and s else None)
                with act.Fori(HT, STEPS) as s:
                    step(s, None, s - 1 if front else None)

            with act.Fori(1, B - 1) as b:
                first_product(b)
                second_product(b, {0: CB - 1})
            first_product(B - 1, front=False)
            second_product(B - 1, {}, front=False)

        @block.vector
        def _(dve):
            def norm_stats(i, b, tile, src, normalised):
                T = TILES * b + tile
                first = isinstance(T, int) and T == 0
                if not first:
                    if not (isinstance(T, int) and T < 2):
                        dve.wait_ge(normalised, T - 1)
                    dve.wait_ge(mv_done[i], T)
                both = 2 * T + 2 if isinstance(T, int) else dve.to_reg(2 * T + 2)
                for h in range(2):
                    nc.vector.bn_stats(stats[:, i, h, :], src[h]).then_inc(bn_done[i], 1)
                dve.wait_ge(s_pool0, 6)
                dve.wait_ge(bn_done[i], both)
                nc.vector.bn_aggr(mv[:, i, tile % 2, :], stats[:, i, :, :].rearrange("p h k -> p (h k)"))\
                    .then_inc(mv_done[i], 1)
                dve.wait_ge(mv_done[i], T + 1)
                nc.vector.tensor_scalar(rstd[:, i, tile % 2, 0:1], mv[:, i, tile % 2, 1:2], EPS, None, ALU.add)\
                    .then_inc(ve_done[i], 1)

            def normalise(i, b, tile, out, src, sem):
                dve.wait_ge(rstd_done[i], TILES * b + tile + 1)
                last = nc.vector.tensor_scalar(out, src, mv[:, i, tile % 2, 0:1], rstd[:, i, tile % 2, 1:2],
                                               ALU.subtract, ALU.mult)
                if sem is not None:
                    last.then_inc(sem, 1)

            def stats_k(b, tile):
                slot, first = tile % 2, isinstance(b, int) and b == 0 and tile < HT
                if first and tile >= 2:
                    dve.wait_ge(xT_landed[slot], 16)
                else:
                    dve.wait_ge(x_landed[slot], 16 * (HT * b + tile // 2 + first))
                at = x_tile(TILES * b + tile, slot)
                norm_stats(0, b, tile, [at[:, 0:512], at[:, 512:H]], xn_ready)

            def norm_k(b, tile):
                at = x_tile(TILES * b + tile, tile % 2)
                normalise(0, b, tile, at, at, xn_ready)

            def stats_x2(b, tile):
                dve.wait_ge(x2t_done, TILES * b + tile + 1)
                norm_stats(1, b, tile, tokens_at(b, tile), xh_ready)

            def norm_x2(b, tile):
                if not (isinstance(b, int) and b == 0 and tile == 0):
                    dve.wait_ge(xt_done, TILES * b + tile)
                if in_acc(b, tile):
                    for h, src in enumerate(tokens_at(b, tile)):
                        normalise(1, b, tile, xh[:, 512 * h:512 * (h + 1)], src, xh_ready if h else None)
                else:
                    normalise(1, b, tile, xh[:, :], trA[:, :, :].rearrange("p c h -> p (c h)"), xh_ready)

            def units(b, pair, slot=None, seen=None):
                if slot is None:
                    slot, seen = pair % 2, pair // 2
                n = UNITS * b + 2 * pair
                first = isinstance(n, int) and n == 0
                u = [2 * pair + j for j in range(2)]
                k = [K[:, u[j], :] for j in range(2)]
                before = [[uOE[:, j, i, 0:HALF] for i in range(2)] for j in range(2)]
                now = [[uOE[:, j, i, 1:] for i in range(2)] for j in range(2)]
                for j in range(2):
                    if not first:
                        dve.wait_ge(y_done, n + j - 1)
                        dve.wait_ge(o_saved, n + j - 1)
                    nc.vector.tensor_copy(uOE[:, j, 0, 0:1], st_o[:, bass.ds(u[j], 1)]).then_inc(o_seeded, 1)
                for j in range(2):
                    nc.vector.tensor_tensor_scan(now[j][0], w_u[:, 0, bass.ds(u[j], 1)].to_broadcast([P, HALF]),
                                                 k[j], st_o[:, bass.ds(u[j], 1)], ALU.add, ALU.max)\
                        .then_inc(o_scanned, 1)
                for j in range(2):
                    dve.wait_ge(o_scanned, n + j + 1)
                    nc.vector.tensor_tensor(now[j][1], k[j], now[j][0], ALU.subtract).then_inc(d1_done, 1)
                    dve.wait_ge(o_seeded, n + j + 1)
                    nc.vector.scalar_tensor_tensor(uA[:, j, :], before[j][0], w_u[:, 0, bass.ds(u[j], 1)],
                                                   now[j][0], ALU.add, ALU.subtract).then_inc(d2_done, 1)
                    if not first:
                        dve.wait_ge(y_done, n + j - 1)
                    nc.vector.scalar_tensor_tensor(uR[:, j, :], k[j], w_u[:, 1, bass.ds(u[j], 1)],
                                                   before[j][0], ALU.add, ALU.subtract).then_inc(z_raw, 1)
                    nc.vector.tensor_copy(st_o[:, bass.ds(u[j] + CB, 1)], uOE[:, j, 0, HALF:]).then_inc(o_saved, 1)
                for j in range(2):
                    dve.wait_ge(z_raw, n + j + 1)
                    nc.vector.tensor_scalar(uR[:, j, :], uR[:, j, :], R_CAP, None, ALU.min).then_inc(z_done, 1)
                for j in range(2):
                    dve.wait_ge(d2_done, n + j + 1)
                    if not first:
                        dve.wait_ge(pq_saved, n + j - 1)
                    nc.vector.tensor_copy(uOE[:, j, :, 0], st_pq[:, u[j], :]).then_inc(pq_seeded, 1)
                for j in range(2):
                    dve.wait_ge(a2_done, n + j + 1)
                    dve.wait_ge(ev_done, n + j + 1)
                    nc.vector.tensor_tensor_scan(now[j][1], uA[:, j, :], now[j][1],
                                                 st_pq[:, u[j], 1:2], ALU.mult, ALU.add).then_inc(q_scanned, 1)
                for j in range(2):
                    nc.vector.tensor_tensor_scan(now[j][0], uA[:, j, :], now[j][0],
                                                 st_pq[:, u[j], 0:1], ALU.mult, ALU.add).then_inc(p_scanned, 1)
                for j in range(2):
                    dve.wait_ge(p_scanned, n + j + 1)
                    nc.vector.tensor_copy(st_pq[:, u[j] + CB, :], uOE[:, j, :, HALF]).then_inc(pq_saved, 1)
                for j in range(2):
                    dve.wait_ge(den_done, n + j + 1)
                    nc.vector.reciprocal(uR[:, j, :], uR[:, j, :]).then_inc(rec_done, 1)
                for j in range(2):
                    dve.wait_ge(rec_done, n + j + 1)
                    dve.wait_ge(num_done, n + j + 1)
                    nc.vector.tensor_tensor(k[j], uV[:, j, :], uR[:, j, :], ALU.mult).then_inc(y_done, 1)
                dve.wait_ge(y_done, n + 2)
                dve.wait_ge(xT_landed[slot], 16 * (HT * b + seen + 2))
                y = K[:, bass.ds(2 * pair, 2), :]
                nc.vector.scalar_tensor_tensor(y, y, tg[:, 0:1], xT2[:, slot, :, :], ALU.mult, ALU.add)\
                    .then_inc(x2_done, 1)

            def add_out(b, s, half):
                dve.wait_ge(acc_drained, GROUPS * b + GROUPS1 + 2 * s + half + 1)
                dve.wait_ge(xo_landed[s % 2], 16 * (CB // 2 * b + s // 2 + 1))
                o = xo[:, s % 2, HALF * half:HALF * (half + 1)]
                nc.vector.scalar_tensor_tensor(o, e16[:, half, :], tg[:, 1:2], o, ALU.mult, ALU.add)\
                    .then_inc(out_added, 1)

            def posts(b, tiles):
                for t in tiles:
                    stats_x2(b, t)
                    norm_x2(b, t)

            stats_k(0, 0)
            for t in range(HT):
                if t + 1 < HT:
                    stats_k(0, t + 1)
                norm_k(0, t)
            dve.wait_ge(s_const, 16 * 8)
            dve.wait_ge(s_pool0, 6)
            dve.wait_ge(k_copied, HT)
            dve.wait_ge(s_tg, 1)
            for pair in range(HT):
                units(0, pair)
            for t in (0, 2):
                stats_x2(0, t)
                stats_k(0, HT + t // 2)
                stats_x2(0, t + 1)
                norm_x2(0, t)
                norm_k(0, HT + t // 2)
                norm_x2(0, t + 1)
            for t in range(HT + 2, TILES):
                stats_k(0, t)
                norm_k(0, t)
            dve.wait_ge(k_copied, TILES)
            for pair in range(HT, 2 * HT):
                units(0, pair)
            posts(0, range(HT, TILES))
            for t in range(TILES):
                stats_k(1, t)
                norm_k(1, t)
            dve.wait_ge(k_copied, 2 * TILES)
            for pair in range(HT):
                units(1, pair)

            def second_product(b, pairs, front=True):
                for s in range(STEPS):
                    if front:
                        stats_x2(b + 1, s)
                    if s >= 1:
                        add_out(b, s - 1, 1)
                    if front:
                        norm_x2(b + 1, s)
                    if s in pairs:
                        units(b + 1, pairs[s])
                    add_out(b, s, 0)

            second_product(0, FRONT_M0)

            def first_product(b, front=True):
                if not front:
                    add_out(b - 1, STEPS - 1, 1)
                    return
                for s in range(HT):
                    stats_k(b + 1, 2 * s)
                    norm_k(b + 1, 2 * s)
                    if s == 0:
                        add_out(b - 1, STEPS - 1, 1)
                    stats_k(b + 1, 2 * s + 1)
                    norm_k(b + 1, 2 * s + 1)
                    if s >= 1:
                        if s == 1:
                            dve.wait_ge(k_copied, TILES * (b + 1) + HT)
                        units(b + 1, s - 1)
                with dve.Fori(1, HT - 1) as i:
                    dve.wait_ge(k_copied, TILES * (b + 2))
                    units(b + 1, 2 * i + 1, 1, i)
                    units(b + 1, 2 * i + 2, 0, i + 1)

            with dve.Fori(1, B - 1) as b:
                first_product(b)
                second_product(b, {0: CB - 1})
            first_product(B - 1, front=False)
            second_product(B - 1, {}, front=False)
            add_out(B - 1, STEPS - 1, 1)

        @block.tensor
        def _(pe):
            def transpose_k(b, tile, slot):
                T = TILES * b + tile
                pe.wait_ge(xn_ready, T + 1)
                if not (isinstance(T, int) and T < 2):
                    pe.wait_ge(k_copied, T - 1 if isinstance(T, int) and T < HT else T)
                    if not (isinstance(b, int) and b == 0 and tile < HT):
                        pe.wait_ge(xh_ready, HT if isinstance(b, int) and b == 0 else TILES * b)
                for c in range(CB):
                    to = acc[2 + c // 4][:, P * (c % 4):P * (c % 4 + 1)] if in_acc(b, tile) else trA[:, c, :]
                    mm = nc.tensor.transpose(to, x_tile(T, slot)[:, P * c:P * (c + 1)], ident[:, :])
                mm.then_inc(kt_done, 1)

            def transpose_x2T(b, tile):
                T = TILES * b + tile
                h = tile // HT
                pe.wait_ge(x2_done, CB * b + HT * (h + 1))
                pe.wait_ge(k_copied, HT if isinstance(T, int) and T < HT else TILES * (b + 1))
                if isinstance(T, int) and T < HT:
                    if T >= 2:
                        pe.wait_ge(xh_ready, T - 1)
                else:
                    pe.wait_ge(xh_ready, T)
                for c in range(CB):
                    to = acc[2 + c // 4][:, P * (c % 4):P * (c % 4 + 1)] if in_acc(b, tile) else trA[:, c, :]
                    mm = nc.tensor.transpose(to, K[:, CB * h + c, P * (tile % HT):P * (tile % HT + 1)],
                                             ident[:, :])
                mm.then_inc(x2t_done, 1)

            def transpose_x2(b, tile):
                T = TILES * b + tile
                pe.wait_ge(xh_ready, T + 1)
                if not (isinstance(T, int) and T == 0):
                    pe.wait_ge(xt_copied, T)
                for c in range(CB):
                    mm = nc.tensor.transpose(trX[:, c, :], xh[:, P * c:P * (c + 1)], ident16[:, :])
                mm.then_inc(xt_done, 1)

            def group1(m, slot, q, half, bank):
                if not (isinstance(m, int) and m < BANKS):
                    pe.wait_ge(acc_drained, m - BANKS + 1)
                for c in range(CB):
                    for part in range(2):
                        mm = nc.tensor.matmul(acc[bank][:, :], W[:, slot, part, q, P * c:P * (c + 1)],
                                              XT[:, c, HALF * half:HALF * (half + 1)],
                                              start=(c == 0 and part == 0), stop=(c == CB - 1 and part == 1))
                mm.then_inc(mm_done, 1)

            def second_product(b, front=True):
                for s in range(STEPS):
                    slot = s % 2
                    split = isinstance(b, int) and b == 0
                    if not split:
                        pe.wait_ge(w_landed[slot], 16 * (Q + CB * (b - 1) + Q + s // 2 + 1))
                    for half in range(2):
                        m = GROUPS * b + GROUPS1 + 2 * s + half
                        bank = (2 * s + half) % BANKS
                        if front and half == 0:
                            transpose_x2T(b + 1, s)
                        pe.wait_ge(acc_drained, m - BANKS + 1)
                        if front and half == 1:
                            transpose_x2(b + 1, s)
                        for q in range(Q):
                            if split and half == 0:
                                pe.wait_ge(lo_done, NB + Q * s + q + 1)
                            if s == 0 and half == 0 and q == Q - 1:
                                pe.wait_ge(acc_drained, GROUPS * b + GROUPS1)
                            for c in range(CB):
                                nb = CB * q + c
                                for part in range(2):
                                    mm = nc.tensor.matmul(
                                        acc[bank][:, :], W[:, slot, part, q, P * c:P * (c + 1)],
                                        DT[:, nb, HALF * half:HALF * (half + 1)],
                                        start=(nb == 0 and part == 0), stop=(nb == NB - 1 and part == 1))
                        mm.then_inc(mm_done, 1)

            pe.wait_ge(s_pool0, 6)
            for t in range(HT):
                transpose_k(0, t, t % 2)
            posts = [("x2T", 0), ("x2T", 1), ("x2", 0), ("x2T", 2), ("x2", 1), ("x2T", 3), ("x2", 2), ("x2", 3)]
            for what, t in posts:
                (transpose_x2T if what == "x2T" else transpose_x2)(0, t)
            transpose_k(0, HT, 0)
            pe.wait_ge(xt_copied, HT)
            for s in range(2):
                for q in range(Q):
                    pe.wait_ge(lo_done, Q * s + q + 1)
                    group1(Q * s + q, s, q, 0, q)
                    if s == 0 and q + 1 < HT:
                        transpose_k(0, HT + q + 1, (q + 1) % 2)

            def split_steps(p, posts_at):
                for slot in range(2):
                    for q in range(Q):
                        m = 2 * Q * p + Q * slot + q
                        pe.wait_ge(lo_done, m + 1)
                        group1(m, slot, q, 0, q)
                        for what, t in posts_at.get((slot, q), ()):
                            (transpose_x2T if what == "x2T" else transpose_x2)(0, t)

            with pe.Fori(1, STEPS // 2 - 1) as p:
                split_steps(p, {})
            split_steps(STEPS // 2 - 1, POSTS_P1)
            transpose_k(1, 0, 0)
            pe.wait_ge(xt_copied, TILES)
            for s in range(2):
                pe.wait_ge(w_landed[s], 16)
                for q in range(Q):
                    group1(NB + Q * s + q, s, q, 1, q)
                    if Q * s + q + 1 < TILES:
                        transpose_k(1, Q * s + q + 1, (q + 1) % 2)
            with pe.Fori(1, STEPS // 2) as p:
                for slot in range(2):
                    pe.wait_ge(w_landed[slot], 16 * p + 16)
                    for q in range(Q):
                        group1(NB + 2 * Q * p + Q * slot + q, slot, q, 1, q)
            second_product(0)

            def first_product(b, front=True):
                pe.wait_ge(xt_copied, TILES * (b + 1))

                def pair_of_steps(p, tiles):
                    for slot in range(2):
                        pe.wait_ge(w_landed[slot], 16 * (Q + CB * (b - 1) + p + 1))
                        for i in range(2 * Q):
                            m = GROUPS * b + 4 * Q * p + 2 * Q * slot + i
                            group1(m, slot, i // 2, i % 2, i % BANKS)
                            if tiles and i in (1, 2):
                                transpose_k(b + 1, 4 * p + 2 * slot + i - 1, i - 1)

                pair_of_steps(0, front)
                pair_of_steps(1, front)
                with pe.Fori(2, STEPS // 2) as p:
                    pair_of_steps(p, False)

            with pe.Fori(1, B - 1) as b:
                first_product(b)
                second_product(b)
            first_product(B - 1, front=False)
            second_product(B - 1, front=False)


V_P1 = {11: 5, 16: 6, 20: 7}
FRONT_P1 = {(0, 3): 4, (1, 3): 5, (3, 0): 6, (4, 1): 7}
FRONT_P2 = {(1, 3): 0, (3, 1): 1, (4, 2): 2, (6, 0): 3}
FRONT_M0 = {0: 4, 1: 5, 2: 6, 3: 7}
POSTS_P1 = {(0, 1): [("x2T", 4)], (0, 2): [("x2", 4), ("x2T", 5)], (1, 0): [("x2", 5), ("x2T", 6)],
            (1, 1): [("x2", 6), ("x2T", 7)], (1, 3): [("x2", 7)]}
LEAD = 7


def kernel(x, ctx_2048, g_xattn, g_ffn, L0_xattn_w, L0_xattn_u, L0_ffn_W0, L0_ffn_bias0, L0_ffn_W1,
           L0_ffn_bias1):
    import concourse.bacc as bacc
    from concourse.bass_utils import run_bass_kernel_spmd

    def blocks(v, n):
        return np.asarray(v).reshape(n, P).T

    def units(v):
        return np.asarray(v).reshape(B, 2, HALF, CB, P).transpose(0, 1, 3, 4, 2).reshape(B, UNITS, P, HALF)

    arrays = {
        "x": np.asarray(x).reshape(B * TILES, P, H),
        "xT": units(x).reshape(B, CB, 2, P, HALF).transpose(0, 1, 3, 2, 4),
        "vT": units(ctx_2048),
        "g_xattn": np.broadcast_to(np.asarray(g_xattn).reshape(1, 1), (P, 1)),
        "g_ffn": np.broadcast_to(np.asarray(g_ffn).reshape(1, 1), (P, 1)),
        "w": blocks(L0_xattn_w, CB),
        "u": blocks(L0_xattn_u, CB),
        "w0": np.asarray(L0_ffn_W0).reshape(NB, P, CB, P).transpose(0, 3, 2, 1).reshape(NB, P, 1024),
        "bias0": blocks(L0_ffn_bias0, NB),
        "w1": np.asarray(L0_ffn_W1).reshape(CB, P, Q, CB, P).transpose(0, 2, 4, 3, 1).reshape(NB, P, 1024),
        "bias1": blocks(L0_ffn_bias1, CB),
    }
    arrays = {n: np.ascontiguousarray(a) for n, a in arrays.items()}
    nc = bacc.Bacc("TRN2", target_bir_lowering=False, num_devices=1)
    args = {n: nc.dram_tensor(f"{n}_in", a.shape, mybir.dt.from_np(a.dtype), kind="ExternalInput").ap()
            for n, a in arrays.items()}
    out = nc.dram_tensor("out", (B, CB, P, L), F32, kind="ExternalOutput").ap()
    build(nc, **args, out=out)
    r = run_bass_kernel_spmd(nc, [{f"{n}_in": a for n, a in arrays.items()}], core_ids=[0])
    return r.results[0]["out"].reshape(B, H, L).transpose(0, 2, 1)
```
